# Optimizing a Trainium2 kernel written in Bass

```python
import numpy as np
import jax
import jax.numpy as jnp

def _softmax(x, axis=-1):
    return jax.nn.softmax(x, axis=axis)

def _gelu(x):
    return jax.nn.gelu(x, approximate=True)

def _silu(x):
    return jax.nn.silu(x)

def _sigmoid(x):
    return jax.nn.sigmoid(x)

def _layernorm(x, axis=-1, eps=1e-05):
    m = jnp.mean(x, axis=axis, keepdims=True)
    v = jnp.var(x, axis=axis, keepdims=True)
    return (x - m) / jnp.sqrt(v + eps)

def _scatter_add(tgt, idx, src, axis=0):
    return tgt.at[idx].add(src)

def _segment_sum(src, seg, n):
    return jax.ops.segment_sum(src, seg, n)
kernel_name = 'mk_lm_tower_d1_tok_ids768_r4_343781'

def setup_inputs(seed: int=0):
    np.random.seed(seed)
    _w = jnp.asarray

    def _rec_inputs():
        import jax
        import jax.numpy as jnp
        _rk = jax.random.key(seed)
        x = jax.random.randint(jax.random.fold_in(_rk, 1), (8, 1024), 0, 12564, jnp.int32)
        return x
    x = _rec_inputs()

    def _L0_tok_setup():
        import jax, jax.numpy as jnp
        import numpy as np
        VOCAB = 50257
        DIM = 192
        B, S = (8, 512)
        key = jax.random.key(seed)
        k1, k2 = jax.random.split(key)
        x = jax.random.randint(k1, (B, S), 0, VOCAB, dtype=jnp.int64 if jax.config.jax_enable_x64 else jnp.int32)
        weight = jax.random.normal(k2, (VOCAB, DIM), dtype=jnp.float32)
        return {'x': x, 'weight': weight}
    _L0_tok_all = _L0_tok_setup()
    _L0_tok_in = {k: v for k, v in _L0_tok_all.items() if k in ('weight',)}
    del _L0_tok_all

    def _L0_attn_setup():
        import jax, jax.numpy as jnp
        import numpy as np
        EMBED_DIM = 192
        SEQ_LEN = 256
        BATCH = 32
        ALPHA = 0.99

        def _decay_mask(sl: int, alpha: float) -> jnp.ndarray:
            i = jnp.arange(sl, dtype=jnp.float32)
            diff = i[:, None] - i[None, :]
            return jnp.where(diff >= 0, jnp.float32(alpha) ** diff, 0.0)
        key = jax.random.key(seed)
        k1, k2 = jax.random.split(key)
        x = jax.random.normal(k1, (BATCH, SEQ_LEN, EMBED_DIM), dtype=jnp.float32)
        W_qkv = jax.random.normal(k2, (EMBED_DIM, 3 * EMBED_DIM), dtype=jnp.float32) * EMBED_DIM ** (-0.5)
        b_qkv = jnp.zeros((3 * EMBED_DIM,), dtype=jnp.float32)
        return {'x': x, 'W_qkv': W_qkv, 'b_qkv': b_qkv}
    _L0_attn_all = _L0_attn_setup()
    _L0_attn_in = {k: v for k, v in _L0_attn_all.items() if k in ('W_qkv', 'b_qkv')}
    del _L0_attn_all

    def _L0_ffn_setup():
        import jax, jax.numpy as jnp
        import numpy as np
        DIM = 192
        NUM_EXPERTS = 8
        TOP_K = 2
        MLP_RATIO = 4
        CAPACITY_RATIO = 1.25
        key = jax.random.key(seed)
        ks = jax.random.split(key, 6)
        B, N, C = (16, 256, DIM)
        H = MLP_RATIO * C
        s_in = 1.0 / np.sqrt(C)
        s_h = 1.0 / np.sqrt(H)
        return {'x': jax.random.normal(ks[0], (B, N, C), dtype=jnp.float32), 'Wg': jax.random.normal(ks[1], (C, NUM_EXPERTS), dtype=jnp.float32) * s_in, 'W1': jax.random.normal(ks[2], (NUM_EXPERTS, C, H), dtype=jnp.float32) * s_in, 'b1': jnp.zeros((NUM_EXPERTS, H), dtype=jnp.float32), 'W2': jax.random.normal(ks[3], (NUM_EXPERTS, H, C), dtype=jnp.float32) * s_h, 'b2': jnp.zeros((NUM_EXPERTS, C), dtype=jnp.float32)}
    _L0_ffn_all = _L0_ffn_setup()
    _L0_ffn_in = {k: v for k, v in _L0_ffn_all.items() if k in ('Wg', 'W1', 'b1', 'W2', 'b2')}
    del _L0_ffn_all
    return {'x': x, 'L0_tok_weight': _L0_tok_in['weight'], 'L0_attn_W_qkv': _L0_attn_in['W_qkv'], 'L0_attn_b_qkv': _L0_attn_in['b_qkv'], 'L0_ffn_Wg': _L0_ffn_in['Wg'], 'L0_ffn_W1': _L0_ffn_in['W1'], 'L0_ffn_b1': _L0_ffn_in['b1'], 'L0_ffn_W2': _L0_ffn_in['W2'], 'L0_ffn_b2': _L0_ffn_in['b2']}

def reference(x, L0_tok_weight, L0_attn_W_qkv, L0_attn_b_qkv, L0_ffn_Wg, L0_ffn_W1, L0_ffn_b1, L0_ffn_W2, L0_ffn_b2):
    import jax
    import jax.numpy as jnp

    def _L0_tok_ref(x, weight):
        import jax, jax.numpy as jnp
        import numpy as np
        VOCAB = 50257
        DIM = 192
        B, S = (8, 512)
        return weight[x]

    def _L0_attn_ref(x, W_qkv, b_qkv):
        import jax, jax.numpy as jnp
        import numpy as np
        EMBED_DIM = 192
        SEQ_LEN = 256
        BATCH = 32
        ALPHA = 0.99

        def _decay_mask(sl: int, alpha: float) -> jnp.ndarray:
            i = jnp.arange(sl, dtype=jnp.float32)
            diff = i[:, None] - i[None, :]
            return jnp.where(diff >= 0, jnp.float32(alpha) ** diff, 0.0)
        bs, sl, d = x.shape
        qkv = x @ W_qkv + b_qkv
        q, k, v = jnp.split(qkv, 3, axis=-1)
        M = _decay_mask(sl, ALPHA)
        dim_sqrt = jnp.sqrt(jnp.float32(d))
        scores = jnp.einsum('bsd,btd->bst', q, k) / dim_sqrt * M
        return jnp.einsum('bst,btd->bsd', scores, v)

    def _L0_ffn_ref(x, Wg, W1, b1, W2, b2):
        import jax, jax.numpy as jnp
        import numpy as np
        DIM = 192
        NUM_EXPERTS = 8
        TOP_K = 2
        MLP_RATIO = 4
        CAPACITY_RATIO = 1.25
        B, N, C = x.shape
        E = W1.shape[0]
        K = TOP_K
        T = B * N
        cap = int(CAPACITY_RATIO * T * K / E)
        xf = x.reshape(T, C)
        logits = xf @ Wg
        topv, topi = jax.lax.top_k(logits, K)
        w = jax.nn.softmax(topv, axis=-1)
        priority = w[:, 0]
        order = jnp.argsort(-priority)
        e_ids = topi[order].reshape(T * K)
        w_ord = w[order].reshape(T * K)
        tok_rep = jnp.repeat(order, K)
        oh = jax.nn.one_hot(e_ids, E, dtype=jnp.int32)
        pos = (jnp.cumsum(oh, axis=0) * oh).sum(-1) - 1
        keep = pos < cap
        slot = jnp.where(keep, e_ids * cap + pos, E * cap)
        buf = jnp.zeros((E * cap + 1, C), xf.dtype).at[slot].set(xf[tok_rep])
        buf_e = buf[:E * cap].reshape(E, cap, C)
        h = jax.nn.gelu(jnp.einsum('ecd,edh->ech', buf_e, W1) + b1[:, None, :], approximate=False)
        out = jnp.einsum('ech,ehd->ecd', h, W2) + b2[:, None, :]
        out_flat = jnp.concatenate([out.reshape(E * cap, C), jnp.zeros((1, C), xf.dtype)], axis=0)
        y_assign = out_flat[slot] * (w_ord * keep.astype(xf.dtype))[:, None]
        y = jnp.zeros((T, C), xf.dtype).at[tok_rep].add(y_assign)
        return y.reshape(B, N, C)
    h = _L0_tok_ref(x, L0_tok_weight)
    h = h + _L0_attn_ref(_layernorm(h, axis=-1), L0_attn_W_qkv, L0_attn_b_qkv)
    h = h + _L0_ffn_ref(_layernorm(h, axis=-1), L0_ffn_Wg, L0_ffn_W1, L0_ffn_b1, L0_ffn_W2, L0_ffn_b2)
    return h

_drawn_inputs = setup_inputs


def setup_inputs(seed=0):
    import zlib

    import numpy as np

    out = dict(_drawn_inputs(seed))
    spreads = {'L0_attn_b_qkv': (0.0, 0.1), 'L0_ffn_b1': (0.0, 0.8), 'L0_ffn_b2': (0.0, 0.8)}
    factors = {}
    for name, (base, spread) in spreads.items():
        noise = np.random.default_rng([zlib.crc32(name.encode()), seed]).standard_normal(out[name].shape)
        drawn = base * np.exp(spread * noise) if base else spread * noise
        out[name] = jnp.asarray(drawn.astype(out[name].dtype))
    for name, factor in factors.items():
        out[name] = (out[name] * factor).astype(out[name].dtype)
    return out
```

```python
from contextlib import ExitStack

import numpy as np
import concourse.bass as bass
from concourse import mybir

ALU = mybir.AluOpType
ACT = mybir.ActivationFunctionType
F32 = mybir.dt.float32
F16 = mybir.dt.float16
I32 = mybir.dt.int32
U32 = mybir.dt.uint32
AX = mybir.AxisListType

P = 128
ALPHA = 0.99
LN_EPS = 1e-5
WSCALE = 64.0
CH = 4
GT = CH * P
TM = 256
META = 8
NCONST = 688

C_ID, C_UP, C_MASK, C_ONE, C_EX, C_REG, C_TOK, C_TAB, C_PAD = 0, 128, 256, 384, 512, 520, 528, 592, 672
C_ROW, C_VAR, C_OUT, C_POW = 674, 675, 676, 678


def constants(T, E, region, ntab):
    c = np.zeros((P, NCONST), np.float64)
    a = float(np.float32(ALPHA))
    s, t = np.arange(P)[:, None], np.arange(P)[None, :]
    c[:, C_ID:C_ID + P] = s == t
    c[:, C_UP:C_UP + P] = s < t
    c[:, C_MASK:C_MASK + P] = np.where(s <= t, a ** -P, 0.0)
    c[:, C_ONE:C_ONE + P] = 1.0
    p = np.arange(P, dtype=np.float64)
    c[:, C_ROW] = a ** (-p / 2)
    c[:, C_VAR] = a ** p
    c[:, C_OUT] = a ** (P + 1.5 * p) / WSCALE
    c[:, C_POW:C_POW + CH] = -0.5
    c[:, C_EX:C_EX + E] = np.arange(E)
    c[:, C_REG:C_REG + E] = np.arange(E) * region
    c[:, C_TOK:C_TOK + T // P] = np.arange(T // P)[None, :] * P + s
    c[:, C_TAB:C_TAB + ntab] = np.arange(ntab)
    c[:, C_PAD:C_PAD + 2] = T + np.arange(2)[None, :] * P + s
    return c.astype(np.float32)


def lm_tower(nc, x, emb, w_qkv, b_qkv, wg, w1, b1, w2, b2, consts, out):
    B, S = x.shape
    T = B * S
    D = emb.shape[1]
    E = wg.shape[1]
    H = w1.shape[2]
    K = 2
    NCH = T // P
    D1 = D - P
    HM = H // P
    HB = HM // 2
    CAP = int(1.25 * T * K / E)
    NT = T * K // TM + E
    NTAB = NT + 2
    REGION = T + TM
    ROW = 2 * D + META
    MF = D
    W1C, W2C = 4 * H, 2 * HM * D
    A128 = float(np.float64(np.float32(ALPHA)) ** P)
    assert S == 2 * GT and D1 == 64 and B == E and NT % 2 == 0 and T + TM == out.shape[0]

    disp = nc.dram_tensor("disp", [E * REGION + TM, ROW // 2], I32, kind="Internal").ap()

    with ExitStack() as ctx:
        def sem(name):
            return ctx.enter_context(nc.semaphore(name))

        def sb(name, shape, dt):
            return ctx.enter_context(nc.sbuf_tensor(name, shape, dt))

        def psum(name, shape, dt):
            return ctx.enter_context(nc.psum_tensor(name, shape, dt))

        ps_t = psum("ps_t", [P, 4, GT], F16)
        ps_q = psum("ps_q", [P, 2, GT], F32)
        ps_p = psum("ps_p", [P, CH, P], F32)
        ps_s = psum("ps_s", [P, 2, 2 * P], F32)
        ps_a = psum("ps_a", [P, 2, 2 * P], F32)
        ps_g = psum("ps_g", [P, 512], F32)
        ps_h = [ps_q[:, 0, :], ps_q[:, 1, :], ps_p[:, :, :].rearrange("p a b -> p (a b)")]
        ps_o = [ps_s[:, 0, 0:D], ps_a[:, 0, 0:D]]
        ps_z = [ps_q[:, n, :].rearrange("p (a t) -> p a t", a=2) for n in range(2)]
        ps_y = [ps_a, ps_p[:, :, :].rearrange("p (c a) t -> p c (a t)", c=2)]
        ps_lg = ps_g[:, 0:CH * E].rearrange("p (c e) -> p c e", e=E)
        ps_pl = ps_g[:, 64:64 + CH * E].rearrange("p (c e) -> p c e", e=E)
        ps_n = ps_g[:, 128:128 + E]

        cst = sb("cst", [P, NCONST], F32)
        ident = cst[:, C_ID:C_ID + P]
        ones = cst[:, C_ONE:C_ONE + P]
        tri = cst[:, C_MASK:C_MASK + P]
        row_scale = cst[:, C_ROW:C_ROW + 1]
        var_scale = cst[:, C_VAR:C_VAR + 1]
        out_scale = cst[:, C_OUT:C_OUT + 1]
        minus_half = cst[:, C_POW:C_POW + CH]
        ident16 = sb("ident16", [P, P], F16)
        upper16 = sb("upper16", [P, P], F16)
        ones16 = sb("ones16", [P, P], F16)
        tok_i = sb("tok_i", [P, NCH], I32)
        x_rows = sb("x_rows", [NCH, P], I32)
        x_rowsf = sb("x_rowsf", [NCH, P], F32)
        ids = sb("ids", [P, NCH], U32)

        wst = sb("wst", [P, 2, 3 * D], F32)
        wlast = sb("wlast", [P, 3 * D], F32)
        wqk_t = sb("wqk_t", [P, 2, 2, 2 * P], F32)
        a_s = sb("a_s", [P, 4, 2 * P], F16)
        v_s = sb("v_s", [P, 4, D], F16)
        g_st = sb("g_st", [P, 2, E], F32)
        g_last = sb("g_last", [P, E], F32)
        g_zero = sb("g_zero", [2, E], F32)
        g_s = sb("g_s", [P, 4, E], F16)

        w1_st = sb("w1_st", [P, 2, H], F32)
        w1_last = sb("w1_last", [P, H], F32)
        w2_st = sb("w2_st", [P, HM * D], F32)
        w1_s = sb("w1_s", [P, E * W1C], F16)
        w2_s = sb("w2_s", [P, E * W2C], F16)
        b2_s = sb("b2_s", [P, E * D], F32)

        idg = [sb(f"idg{u}", [P, CH], U32) for u in range(2)]
        h = [sb(f"h{u}", [P, CH, D], F32) for u in range(2)]
        xn = [sb(f"xn{u}", [P, CH, D], F32) for u in range(2)]
        xs = [sb(f"xs{u}", [P, CH, 2 * D], F16) for u in range(2)]
        xt = [sb(f"xt{u}", [P, 3, GT], F16) for u in range(2)]
        st = [sb(f"st{n}", [P, CH, 6], F32) for n in range(2)]
        mv = [sb(f"mv{n}", [P, CH, 2], F32) for n in range(2)]
        var = [sb(f"var{n}", [P, CH], F32) for n in range(2)]
        rstd = [sb(f"rstd{n}", [P, CH], F32) for n in range(2)]
        qzs = sb("qzs", [P, 8, GT], F16)
        qs, zs = qzs[:, 0:4, :], qzs[:, 4:8, :]
        pt = sb("pt", [P, CH, P], F32)
        ps = sb("ps", [P, 2, CH, P], F16)
        s32 = sb("s32", [P, 2, D], F32)
        ss = [sb(f"ss{c}", [P, 4, 2 * P], F16) for c in range(CH)]
        h2 = [sb(f"h2{u}", [P, CH, D], F32) for u in range(2)]
        x2n = sb("x2n", [P, CH, D], F32)
        x2s = [sb(f"x2s{u}", [P, CH, ROW], F16) for u in range(2)]
        x2f = [x2s[u][:, :, :].rearrange("p c r -> p (c r)").bitcast(F32).rearrange("p (c r) -> p c r", c=CH) for u in range(2)]
        x2i = [x2s[u][:, :, :].rearrange("p c r -> p (c r)").bitcast(I32).rearrange("p (c r) -> p c r", c=CH) for u in range(2)]
        x2t = sb("x2t", [P, 3, GT], F16)
        lg = sb("lg", [P, CH, E], F32)
        top = sb("top", [P, CH, 8], F32)
        topi = sb("topi", [P, CH, 8], U32)
        topf = sb("topf", [P, 2, CH], F32)
        hot = sb("hot", [P, 2, CH, E], F32)
        hot16 = sb("hot16", [P, CH, E], F16)
        hotsum = sb("hotsum", [P, E], F32)
        hotred = sb("hotred", [P, E], F32)
        hotsum16 = sb("hotsum16", [P, E], F16)
        gap = sb("gap", [P, CH], F32)
        egap = sb("egap", [P, CH], F32)
        egap1 = sb("egap1", [P, CH], F32)
        place = sb("place", [P, CH, E], F32)
        placed = sb("placed", [P, 2, CH, E], F32)
        slotf = sb("slotf", [P, 2, CH], F32)
        slot = [sb(f"slot{u}", [P, 2, CH], U32) for u in range(2)]
        prio = sb("prio", [P, NCH], F32)
        assigned = sb("assigned", [P, NCH * E], F32)

        cnt = sb("cnt", [P, E], F32)
        padf = sb("padf", [P, E], F32)
        pad_i = sb("pad_i", [P, E], I32)
        tiles_i = sb("tiles_i", [P, E], I32)
        tiles_f = sb("tiles_f", [P, E], F32)
        ends = sb("ends", [P, E], F32)
        past = h[1][:, :, :].rearrange("p a b -> p (a b)")[:, 0:NTAB * E].rearrange("p (a b) -> p a b", b=E)
        prod = x2n[:, :, :].rearrange("p a b -> p (a b)")[:, 0:NTAB * E].rearrange("p (a b) -> p a b", b=E)
        tab_e = sb("tab_e", [P, NTAB], F32)
        tab_ew = sb("tab_ew", [P, NTAB], F32)
        tab_start = sb("tab_start", [P, NTAB], F32)
        tab_off = sb("tab_off", [P, NTAB], F32)
        tab_offv = sb("tab_offv", [P, NTAB], F32)
        tab_row0 = sb("tab_row0", [P, NTAB], F32)
        tab_row = sb("tab_row", [P, NTAB], F32)
        tab_row_i = sb("tab_row_i", [P, NTAB], I32)
        tab_e_i = sb("tab_e_i", [P, NTAB], I32)
        tab = sb("tab", [P, NTAB, 4], F32)
        over = sb("over", [P, 2], F32)
        over_i = sb("over_i", [P, 1], I32)
        limit = sb("limit", [P, E], F32)
        limit_tok = sb("limit_tok", [P, E], F32)
        pm = xn[0][:, :, :].rearrange("p a b -> p (a b)")[:, 0:E * NCH].rearrange("p (a b) -> p a b", b=NCH)
        tie = xn[1][:, :, :].rearrange("p a b -> p (a b)")[:, 0:E * NCH].rearrange("p (a b) -> p a b", b=NCH)
        cmp = h[0][:, :, :].rearrange("p a b -> p (a b)")[:, 0:E * NCH].rearrange("p (a b) -> p a b", b=NCH)
        part_cnt = sb("part_cnt", [P, E], F32)
        cand = sb("cand", [P, E], F32)
        took = sb("took", [P, E], F32)
        room = sb("room", [P, E], F32)
        move = sb("move", [P, 2], F32)
        pad_rows = sb("pad_rows", [P, 2, ROW], F16)
        pad_u = pad_rows[:, :, :].rearrange("p c r -> p (c r)").bitcast(I32).rearrange("p (c r) -> p c r", c=2)

        out_zero = w1_st[:, 0, 0:2 * D].rearrange("p (c d) -> p c d", c=2)

        tview = ps_t[:, 0:2, :].rearrange("p a b -> p (a b)")[:, 0:3 * TM].rearrange("p (a b) -> p a b", b=TM)
        xrow = [sb(f"xrow{u}", [P, 2, ROW], F16) for u in range(2)]
        xrf = [xrow[u][:, :, :].rearrange("p c r -> p (c r)").bitcast(F32).rearrange("p (c r) -> p c r", c=2) for u in range(2)]
        xru = [xrow[u][:, :, :].rearrange("p c r -> p (c r)").bitcast(U32).rearrange("p (c r) -> p c r", c=2) for u in range(2)]
        xri = [xrow[u][:, :, :].rearrange("p c r -> p (c r)").bitcast(I32).rearrange("p (c r) -> p c r", c=2) for u in range(2)]
        xtt = x2t[:, :, 0:TM]
        h32 = w1_st[:, :, :].rearrange("p a b -> p (a b)").rearrange("p (a b) -> p a b", b=TM)
        hs = qzs[:, :, :].rearrange("p a b -> p (a b)")[:, 0:2 * HM * TM].rearrange("p (v m b) -> p v m b", v=2, b=TM)
        osum = [h2[u][:, 0:2, :] for u in range(2)]
        oy = [h2[u][:, 2:4, :] for u in range(2)]
        tinfo = sb("tinfo", [P, 4], F32)
        dest = [sb(f"dest{u}", [P, 2], U32) for u in range(2)]
        wk = sb("wk", [P, 7, 2], F32)
        wfin = [sb(f"wfin{u}", [P, 2], F32) for u in range(2)]

        s_c_ld = sem("c_ld")
        s_c_up = sem("c_up")
        s_c_16 = sem("c_16")
        s_c_init = sem("c_init")
        s_x_ld = sem("x_ld")
        s_xf_ok = sem("xf_ok")
        s_xtr_full = sem("xtr_full")
        s_ids_ok = sem("ids_ok")
        s_w_ld = sem("w_ld")
        s_w_sub = sem("w_sub")
        s_w_bias = sem("w_bias")
        s_w_tr = sem("w_tr")
        s_w_trc = sem("w_trc")
        s_w_a = sem("w_a")
        s_w_ah = sem("w_ah")
        s_w_al = sem("w_al")
        s_v_h = sem("v_h")
        s_v_l = sem("v_l")
        s_g_ld = sem("g_ld")
        s_g_z = sem("g_z")
        s_g_sub = sem("g_sub")
        s_g_bias = sem("g_bias")
        s_g_h = sem("g_h")
        s_g_l = sem("g_l")
        s_b2_ld = sem("b2_ld")
        s_idg_ok = sem("idg_ok")
        s_bn_ok = sem("bn_ok")
        s_mv_ok = sem("mv_ok")
        s_rstd_ok = sem("rstd_ok")
        s_xn_ok = sem("xn_ok")
        s_xh_ok = sem("xh_ok")
        s_xl_ok = sem("xl_ok")
        s_tp_full = sem("tp_full")
        s_tp_a = sem("tp_a")
        s_tp_d = sem("tp_d")
        s_q_full = sem("q_full")
        s_qh_ok = sem("qh_ok")
        s_ql_ok = sem("ql_ok")
        s_p_full = sem("p_full")
        s_pt_ok = sem("pt_ok")
        s_ph_ok = sem("ph_ok")
        s_pl_ok = sem("pl_ok")
        s_s_full = sem("s_full")
        s_s32_ok = sem("s32_ok")
        s_sh_ok = sem("sh_ok")
        s_sl_ok = sem("sl_ok")
        s_zh_ok = sem("zh_ok")
        s_zl_ok = sem("zl_ok")
        s_a_full = sem("a_full")
        s_h2_ok = sem("h2_ok")
        s_bn2_ok = sem("bn2_ok")
        s_mv2_ok = sem("mv2_ok")
        s_rstd2_ok = sem("rstd2_ok")
        s_x2n_ok = sem("x2n_ok")
        s_x2h_ok = sem("x2h_ok")
        s_x2l_ok = sem("x2l_ok")
        s_tp2_full = sem("tp2_full")
        s_tp2_a = sem("tp2_a")
        s_tp2_d = sem("tp2_d")
        s_lg_full = sem("lg_full")
        s_lg_ok = sem("lg_ok")
        s_top_ok = sem("top_ok")
        s_topi_ok = sem("topi_ok")
        s_topf_ok = sem("topf_ok")
        s_hot_ok = sem("hot_ok")
        s_hot16_ok = sem("hot16_ok")
        s_gap_ok = sem("gap_ok")
        s_egap_ok = sem("egap_ok")
        s_eg1_ok = sem("eg1_ok")
        s_wt_ok = sem("wt_ok")
        s_hred_ok = sem("hred_ok")
        s_hsum_ok = sem("hsum_ok")
        s_hs16_ok = sem("hs16_ok")
        s_pl_full = sem("pl_full")
        s_place_ok = sem("place_ok")
        s_placed_ok = sem("placed_ok")
        s_slotf_ok = sem("slotf_ok")
        s_slot_ok = sem("slot_ok")
        s_e_ld = sem("e_ld")
        s_e_sub = sem("e_sub")
        s_e_bias = sem("e_bias")
        s_e_h1 = sem("e_h1")
        s_e_l1 = sem("e_l1")
        s_e_h2 = sem("e_h2")
        s_e_l2 = sem("e_l2")
        s_pad_tok = sem("pad_tok")
        s_pad_st = sem("pad_st")
        s_n_full = sem("n_full")
        s_m_ok = sem("m_ok")
        s_pad_ok = sem("pad_ok")
        s_over_ok = sem("over_ok")
        s_b_part = sem("b_part")
        s_b_tot = sem("b_tot")
        s_b_ok = sem("b_ok")
        s_tab_ok = sem("tab_ok")
        s_t_x = sem("t_x")
        s_t_h = sem("t_h")
        s_t_gelu = sem("t_gelu")
        s_t_hh = sem("t_hh")
        s_t_hl = sem("t_hl")
        s_t_o = sem("t_o")
        s_t_osum = sem("t_osum")
        s_t_oy = sem("t_oy")
        s_t_info = sem("t_info")
        s_t_dest = sem("t_dest")
        s_settled = sem("settled")
        s_z_done = sem("z_done")
        s_z_pad = sem("z_pad")
        s_t_w = sem("t_w")
        s_t_tp = sem("t_tp")
        s_n_ok = sem("n_ok")
        s_var_ok = sem("var_ok")
        s_var2_ok = sem("var2_ok")
        h_ld = [ctx.enter_context(nc.semaphore(f"h_ld{u}")) for u in range(2)]
        out_st = [ctx.enter_context(nc.semaphore(f"out_st{u}")) for u in range(2)]
        slot_st = [ctx.enter_context(nc.semaphore(f"slot_st{u}")) for u in range(2)]
        row_ld = [ctx.enter_context(nc.semaphore(f"row_ld{u}")) for u in range(2)]
        out_add = ctx.enter_context(nc.semaphore("out_add"))
        pad_ld = ctx.enter_context(nc.semaphore("pad_ld"))

        PASSES = ((0, 0), (0, 2), (2, 0), (1, 1), (3, 1))
        PASSES6 = ((0, 0), (0, 2), (2, 0), (1, 1), (1, 3), (3, 1))

        def settle(eng):
            eng.sem_inc(s_settled, 1)

        block = ctx.enter_context(nc.Block())

        def ge(eng, semaphore, value):
            if isinstance(value, int) and value <= 0:
                return
            eng.wait_ge(semaphore, value)

        def pipeline(eng, step):
            step(-1, 1, -1, True, False, False, None)
            step(0, 0, 0, True, True, False, 0)
            with eng.Fori(0, B - 1) as i:
                step(2 * i + 1, 1, i, True, True, True, i + 1)
                step(2 * i + 2, 0, i + 1, True, True, True, None)
            step(2 * B - 1, 1, B - 1, False, True, True, None)
            step(2 * B, 0, B, False, False, True, None)

        ADD_FREE = 64
        FREE = 16

        @block.sync
        def _(sp):
            sp.dma_start(cst[:, :], consts).then_inc(s_c_ld, 16)
            sp.dma_start(x_rows[:, :], x.rearrange("b (r p) -> (b r) p", p=P)).then_inc(s_x_ld, 16)
            sp.dma_start(wst[:, 0, :], w_qkv[0:P, :]).then_inc(s_w_ld, 16)
            sp.dma_start(wst[0:D1, 1, :], w_qkv[P:D, :]).then_inc(s_w_ld, 16)
            sp.dma_start(wst[D1:P, 1, :], w_qkv[P:D, :]).then_inc(s_w_ld, 16)
            sp.dma_start(wlast[:, :], w_qkv[D - 1:D, :].to_broadcast([P, 3 * D])).then_inc(s_w_ld, 16)
            for u in range(2):
                sp.sem_inc(out_st[u], FREE)
            sp.wait_ge(s_w_sub, 2)
            for r in (D1 - 1, P - 1):
                sp.dma_start(wst[r:r + 1, 1, :], b_qkv.rearrange("(a n) -> a n", a=1)).then_inc(s_w_bias, 16)
            sp.dma_start(g_st[:, 0, :], wg[0:P, :]).then_inc(s_g_ld, 16)
            sp.dma_start(g_st[0:D1, 1, :], wg[P:D, :]).then_inc(s_g_ld, 16)
            sp.dma_start(g_st[D1:P, 1, :], wg[P:D, :]).then_inc(s_g_ld, 16)
            sp.dma_start(g_last[:, :], wg[D - 1:D, :].to_broadcast([P, E])).then_inc(s_g_ld, 16)
            sp.wait_ge(s_g_sub, 2)
            sp.wait_ge(s_g_z, 1)
            for r in (D1 - 1, P - 1):
                sp.dma_start(g_st[r:r + 1, 1, :], g_zero[0:1, :]).then_inc(s_g_bias, 16)
            for e in range(E):
                sp.dma_start(b2_s[:, e * D:(e + 1) * D], b2[e:e + 1, :].to_broadcast([P, D])).then_inc(s_b2_ld, 16)

            def step(g, u, b, rows, attend, route, expert):
                if expert is not None:
                    e = expert
                    ge(sp, s_e_l1, e)
                    ge(sp, s_e_l2, e)
                    sp.dma_start(w1_st[:, 0, :], w1[bass.ds(e, 1), 0:P, :].rearrange("e p n -> (e p) n"))\
                        .then_inc(s_e_ld, 16)
                    sp.dma_start(w1_st[0:D1, 1, :], w1[bass.ds(e, 1), P:D, :].rearrange("e p n -> (e p) n"))\
                        .then_inc(s_e_ld, 16)
                    sp.dma_start(w1_st[D1:P, 1, :], w1[bass.ds(e, 1), P:D, :].rearrange("e p n -> (e p) n"))\
                        .then_inc(s_e_ld, 16)
                    sp.dma_start(w1_last[:, :], w1[bass.ds(e, 1), D - 1, :].to_broadcast([P, H])).then_inc(s_e_ld, 16)
                    sp.dma_start(w2_st[:, :].rearrange("p (m n) -> p m n", m=HM),
                                 w2[bass.ds(e, 1), :, :].rearrange("e (m p) n -> p (e m) n", p=P)).then_inc(s_e_ld, 16)
                    sp.wait_ge(s_e_sub, 2 * e + 2)
                    for r in (D1 - 1, P - 1):
                        sp.dma_start(w1_st[r:r + 1, 1, :], b1[bass.ds(e, 1), :]).then_inc(s_e_bias, 16)
                if attend:
                    sp.wait_ge(s_h2_ok, CH * g + CH)
                    sp.dma_start(out[bass.ds(g * GT, GT), :].rearrange("(c p) d -> p c d", p=P),
                                 h2[u][:, :, :]).then_inc(out_st[u], 16)

            sp.wait_ge(out_add, ADD_FREE)
            pipeline(sp, step)

            sp.wait_ge(s_pad_ok, 1)
            for u in range(2):
                sp.wait_ge(slot_st[u], 16 * K * CH * B + FREE)
            for e in range(E):
                first = sp.value_load(pad_i[0:1, e:e + 1], min_val=e * REGION, max_val=e * REGION + T)
                sp.dma_start(disp[bass.ds(first, TM), :].rearrange("(h p) c -> p h c", p=P),
                             pad_u).then_inc(pad_ld, 16)
            sp.wait_ge(pad_ld, 16 * E)
            sp.wait_ge(s_m_ok, 1)

            with sp.Fori(0, NTAB // 2) as i:
                for u in range(2):
                    sp.wait_ge(s_t_tp, 2 * i + u + 1)
                    sp.wait_ge(s_t_w, 2 * i + u + 1)
                    first = sp.value_load(tab_row_i[0:1, bass.ds(2 * i + u, 1)], min_val=0, max_val=E * REGION)
                    sp.dma_start(xri[u], disp[bass.ds(first, TM), :].rearrange("(h p) c -> p h c", p=P))\
                        .then_inc(row_ld[u], 16)
            for u in range(2):
                sp.wait_ge(row_ld[u], 16 * (NTAB // 2))
            sp.wait_ge(out_add, 32 * NT + ADD_FREE)

        @block.gpsimd
        def _(pool):
            pool.memset(g_zero[:, :], 0.0).then_inc(s_g_z, 1)
            pool.memset(out_zero[:, :, :], 0.0).then_inc(s_z_pad, 1)
            pool.memset(pad_rows[:, :, :], 0.0).then_inc(s_pad_tok, 1)
            pool.wait_ge(s_pad_tok, 1)
            pool.wait_ge(s_z_pad, 1)
            pool.wait_ge(s_c_ld, 16)
            pool.tensor_copy(pad_u[:, :, MF], cst[:, C_PAD:C_PAD + 2]).then_inc(s_pad_tok, 1)
            pool.wait_ge(s_pad_tok, 2)
            for u in range(2):
                pool.dma_start(disp[E * REGION + u * P:E * REGION + (u + 1) * P, :], pad_u[:, u, :])\
                    .then_inc(slot_st[u], FREE)
            for q in range(ADD_FREE // 16):
                pool.dma_start(out[T + q * D1:T + (q + 1) * D1, :], out_zero[0:D1, 0, :]).then_inc(out_add, 16)

            def gather(g, u, b):
                ge(pool, h_ld[u], 16 * CH * b)
                settle(pool)
                pool.tensor_copy(idg[u][:, :], ids[:, bass.ds(g * CH, CH)]).then_inc(s_idg_ok, 1)
                pool.wait_ge(s_idg_ok, g + 1)
                ge(pool, s_h2_ok, CH * (g - 1))
                settle(pool)
                for c in range(CH):
                    pool.indirect_dma_start(h[u][:, c, :], None, emb[:, :],
                                            bass.IndirectOffsetOnAxis(ap=idg[u][:, c:c + 1], axis=0))\
                        .then_inc(h_ld[u], 16)

            def deviation(g, n):
                mv_ok, var_ok, rstd_ok = ((s_mv_ok, s_var_ok, s_rstd_ok), (s_mv2_ok, s_var2_ok, s_rstd2_ok))[n]
                pool.wait_ge(mv_ok, CH * g + CH)
                settle(pool)
                pool.tensor_scalar(var[n][:, :], mv[n][:, :, 1], LN_EPS, (var_scale, 1.0)[n], ALU.add, ALU.mult)\
                    .then_inc(var_ok, 1)
                pool.wait_ge(var_ok, g + 1)
                pool.tensor_tensor(rstd[n][:, :], var[n][:, :], minus_half, ALU.pow).then_inc(rstd_ok, 1)

            def low_rows(g, u):
                pool.wait_ge(s_xh_ok, g + 1)
                pool.tensor_tensor(xs[u][:, :, 2 * P:3 * P], xn[u][:, :, 0:P], xs[u][:, :, 0:P], ALU.subtract)\
                    .then_inc(s_xl_ok, 1)
                pool.tensor_tensor(xs[u][:, :, D:D + D1 - 1], xn[u][:, :, P:D - 1], xs[u][:, :, P:D - 1],
                                   ALU.subtract).then_inc(s_xl_ok, 1)

            def low_state(b, k):
                pool.wait_ge(s_sh_ok, 7 * b + k + 1)
                pool.tensor_tensor(ss[k % CH][:, 2:4, 0:D], s32[:, :, :], ss[k % CH][:, 0:2, 0:D], ALU.subtract)\
                    .then_inc(s_sl_ok, 1)

            def scatter(u, k, chunks):
                for c in chunks:
                    pool.indirect_dma_start(disp[:, :], bass.IndirectOffsetOnAxis(ap=slot[u][:, k, c:c + 1], axis=0),
                                            x2i[u][:, c, :], None).then_inc(slot_st[u], 16)

            def step(g, u, b, rows, attend, route, expert):
                v = 1 - u
                if route:
                    deviation(g - 1, 1)
                if rows:
                    gather(g + 1, v, b + u)
                if attend:
                    for k in range(4 * u, min(4 * u + 4, 7)):
                        low_state(b, k)
                if rows:
                    deviation(g + 1, 0)
                if route:
                    pool.wait_ge(s_x2l_ok, 2 * g)
                    pool.wait_ge(s_wt_ok, 5 * g)
                    pool.wait_ge(s_slot_ok, g)
                    settle(pool)
                    scatter(v, 0, range(0, 2))
                if rows:
                    low_rows(g + 1, v)
                if route:
                    scatter(v, 0, range(2, CH))
                    scatter(v, 1, range(CH))

            pool.wait_ge(s_ids_ok, 1)
            pipeline(pool, step)

            for u in range(2):
                pool.wait_ge(out_st[u], 16 * B + FREE)
            with pool.Fori(0, NT // 2) as i:
                for u in range(2):
                    j = 2 * i + u
                    pool.wait_ge(row_ld[u], 16 * i + 16)
                    pool.wait_ge(s_t_osum, 2 * j + 4)
                    pool.wait_ge(s_t_w, j + 3)
                    settle(pool)
                    for b in range(2):
                        pool.tensor_scalar(oy[u][:, b, :], osum[u][:, b, :], wfin[u][:, b:b + 1], None, ALU.mult)\
                            .then_inc(s_t_oy, 1)
                    pool.wait_ge(s_t_oy, 2 * j + 6)
                    pool.wait_ge(out_add, 32 * j + ADD_FREE)
                    settle(pool)
                    for b in range(2):
                        pool.indirect_dma_start(out[:, :], bass.IndirectOffsetOnAxis(ap=dest[u][:, b:b + 1], axis=0),
                                                oy[u][:, b, :], None, compute_op=ALU.add).then_inc(out_add, 16)

        @block.scalar
        def _(act):
            act.wait_ge(s_w_bias, 32)
            act.activation(v_s[:, 0:2, :], wst[:, :, 2 * D:3 * D], ACT.Copy, scale=WSCALE).then_inc(s_v_h, 1)
            act.wait_ge(s_w_a, 1)
            act.activation(a_s[:, 0:2, :], ps_q[:, :, 0:2 * P], ACT.Copy, scale=WSCALE / D ** 0.5).then_inc(s_w_ah, 1)
            act.wait_ge(s_g_bias, 32)
            act.activation(g_s[:, 0:2, :], g_st[:, :, :], ACT.Copy, scale=WSCALE).then_inc(s_g_h, 1)

            def step(g, u, b, rows, attend, route, expert):
                v = 1 - u
                states = list(range(4 * u, min(4 * u + 4, 7)))

                def state(k):
                    act.wait_ge(s_s32_ok, 7 * b + k + 1)
                    act.copy(ss[k % CH][:, 0:2, 0:D], s32[:, :, :]).then_inc(s_sh_ok, 1)

                if attend:
                    ge(act, s_z_done, CH * g)
                    for a in range(2):
                        act.wait_ge(s_q_full, 2 * g + a + 1)
                        act.activation(qs[:, a, :], ps_q[:, a, :], ACT.Copy, scale=1.0 / WSCALE).then_inc(s_qh_ok, 1)
                    state(states[0])
                if route:
                    act.wait_ge(s_x2n_ok, CH * g)
                    act.wait_ge(slot_st[v], 16 * K * CH * (b - 1 + u) + FREE)
                    act.activation(x2s[v][:, :, 0:D - 1], x2n[:, :, 0:D - 1], ACT.Copy).then_inc(s_x2h_ok, 1)
                if attend:
                    state(states[1])
                if route:
                    act.wait_ge(s_tp2_full, g)
                    act.copy(x2t[:, :, :], ps_t[:, 0:3, :]).then_inc(s_tp2_a, 1)
                if attend:
                    state(states[2])
                    for a in range(2):
                        act.wait_ge(s_pt_ok, 2 * g + a + 1)
                        act.copy(ps[:, 0, 2 * a:2 * a + 2, :], pt[:, 2 * a:2 * a + 2, :]).then_inc(s_ph_ok, 1)
                    for k in states[3:]:
                        state(k)
                if route:
                    act.wait_ge(s_gap_ok, g)
                    act.activation(egap[:, :], gap[:, :], ACT.Exp, scale=1.0 / WSCALE).then_inc(s_egap_ok, 1)
                if rows:
                    act.wait_ge(s_xn_ok, CH * g + 2 * CH)
                    ge(act, s_z_done, CH * g)
                    act.activation(xs[v][:, :, 0:D - 1], xn[v][:, :, 0:D - 1], ACT.Copy).then_inc(s_xh_ok, 1)
                if attend:
                    ge(act, s_a_full, 2 * g)
                    for a in range(2):
                        act.wait_ge(s_z_done, CH * g + 2 * a + 2)
                        act.copy(zs[:, 0:2, 2 * a * P:2 * (a + 1) * P], ps_z[a])\
                            .then_inc(s_zh_ok, 1)
                if rows:
                    act.wait_ge(s_tp_full, g + 2)
                    act.copy(xt[v][:, :, :], ps_t[:, 0:3, :]).then_inc(s_tp_a, 1)
                if expert is not None:
                    e = expert
                    act.wait_ge(s_e_bias, 32 * e + 32)
                    act.activation(w1_s[:, bass.ds(e * W1C, 2 * H)], w1_st[:, :, :].rearrange("p a n -> p (a n)"),
                                   ACT.Copy, scale=WSCALE).then_inc(s_e_h1, 1)
                    act.activation(w2_s[:, bass.ds(e * W2C, HM * D)], w2_st[:, :], ACT.Copy, scale=WSCALE)\
                        .then_inc(s_e_h2, 1)

            pipeline(act, step)

            with act.Fori(0, NT) as j:
                for m in range(HB):
                    act.wait_ge(s_t_h, HB * j + m + 1)
                    act.activation(h32[:, 2 * m:2 * m + 2, :].rearrange("p a b -> p (a b)"), ps_h[m], ACT.Gelu,
                                   scale=1.0 / WSCALE).then_inc(s_t_gelu, 1)
                    act.activation(hs[:, 0, 2 * m:2 * m + 2, :].rearrange("p a b -> p (a b)"), ps_h[m], ACT.Gelu,
                                   scale=1.0 / WSCALE).then_inc(s_t_hh, 1)

        @block.vector
        def _(dve):
            dve.wait_ge(s_x_ld, 16)
            dve.tensor_copy(x_rowsf[:, :], x_rows[:, :]).then_inc(s_xf_ok, 1)
            dve.wait_ge(s_c_ld, 16)
            dve.tensor_copy(ident16[:, :], ident).then_inc(s_c_16, 1)
            dve.tensor_copy(upper16[:, :], cst[:, C_UP:C_UP + P]).then_inc(s_c_16, 1)
            dve.tensor_copy(ones16[:, :], ones).then_inc(s_c_16, 1)
            dve.tensor_copy(tok_i[:, :], cst[:, C_TOK:C_TOK + NCH]).then_inc(s_c_init, 1)
            dve.memset(hotsum[:, :], 0.0).then_inc(s_c_init, 1)
            dve.memset(hotsum16[:, :], 0.0).then_inc(s_c_init, 1)
            for u in range(2):
                for c in range(CH):
                    dve.tensor_copy(xn[u][:, c, D - 1:D], row_scale).then_inc(s_c_init, 1)
                dve.memset(x2s[u][:, :, D - 1:D], 1.0).then_inc(s_c_init, 1)
                dve.memset(x2s[u][:, :, 2 * P - 1:2 * P], 0.0).then_inc(s_c_init, 1)
            for c in range(CH):
                dve.memset(ss[c][:, :, :], 0.0).then_inc(s_c_init, 1)
            NINIT = 3 + 2 * (CH + 2) + CH
            dve.wait_ge(s_c_init, NINIT)
            for u in range(2):
                dve.tensor_copy(xs[u][:, :, D - 1:D], xn[u][:, :, D - 1:D]).then_inc(s_c_init, 1)
                dve.wait_ge(s_c_init, NINIT + 2 * u + 1)
                dve.tensor_tensor(xs[u][:, :, 2 * P - 1:2 * P], xn[u][:, :, D - 1:D], xs[u][:, :, D - 1:D], ALU.subtract)\
                    .then_inc(s_c_init, 1)
            dve.wait_ge(s_xtr_full, 1)
            dve.tensor_copy(ids[:, :], ps_g[:, 0:NCH]).then_inc(s_ids_ok, 1)
            dve.wait_ge(s_w_ld, 64)
            for b in range(2):
                dve.tensor_tensor(wst[:, b, :], wst[:, b, :], wlast[:, :], ALU.subtract).then_inc(s_w_sub, 1)
            dve.wait_ge(s_w_tr, 1)
            for t in range(2):
                for m in range(2):
                    r = (P, D1)[m]
                    dve.tensor_copy(wqk_t[0:r, t, m, 0:D], ps_q[0:r, t, m * 2 * P:m * 2 * P + D]).then_inc(s_w_trc, 1)
                    dve.tensor_copy(wqk_t[0:r, t, m, D:2 * P], ps_q[0:r, t, m * 2 * P + P:m * 2 * P + D])\
                        .then_inc(s_w_trc, 1)
            dve.wait_ge(s_v_h, 1)
            dve.scalar_tensor_tensor(v_s[:, 2:4, :], wst[:, :, 2 * D:3 * D], WSCALE, v_s[:, 0:2, :],
                                     ALU.mult, ALU.subtract).then_inc(s_v_l, 1)
            dve.wait_ge(s_w_ah, 1)
            dve.scalar_tensor_tensor(a_s[:, 2:4, :], ps_q[:, :, 0:2 * P], WSCALE / D ** 0.5, a_s[:, 0:2, :],
                                     ALU.mult, ALU.subtract).then_inc(s_w_al, 1)
            dve.wait_ge(s_g_ld, 64)
            for b in range(2):
                dve.tensor_tensor(g_st[:, b, :], g_st[:, b, :], g_last[:, :], ALU.subtract).then_inc(s_g_sub, 1)
            dve.wait_ge(s_g_h, 1)
            dve.scalar_tensor_tensor(g_s[:, 2:4, :], g_st[:, :, :], WSCALE, g_s[:, 0:2, :],
                                     ALU.mult, ALU.subtract).then_inc(s_g_l, 1)

            def statistics(g, n, src):
                bn_ok, mv_ok = ((s_bn_ok, s_mv_ok), (s_bn2_ok, s_mv2_ok))[n]
                for c in range(CH):
                    dve.bn_stats(st[n][:, c, :], src[:, c, :]).then_inc(bn_ok, 1)
                for c in range(CH):
                    dve.wait_ge(bn_ok, CH * g + c + 1)
                    settle(dve)
                    dve.bn_aggr(mv[n][:, c, :], st[n][:, c, :]).then_inc(mv_ok, 1)

            def normalise(g, n, src, dst):
                rstd_ok, xn_ok = ((s_rstd_ok, s_xn_ok), (s_rstd2_ok, s_x2n_ok))[n]
                dve.wait_ge(rstd_ok, g + 1)
                for c in range(CH):
                    dve.tensor_scalar(dst[:, c, 0:D - 1], src[:, c, 0:D - 1], mv[n][:, c, 0:1], rstd[n][:, c:c + 1],
                                      ALU.subtract, ALU.mult).then_inc(xn_ok, 1)

            def experts(e):
                dve.wait_ge(s_e_ld, 80 * e + 80)
                for b in range(2):
                    dve.tensor_tensor(w1_st[:, b, :], w1_st[:, b, :], w1_last[:, :], ALU.subtract).then_inc(s_e_sub, 1)

            def experts_low(e):
                dve.wait_ge(s_e_h1, e + 1)
                dve.scalar_tensor_tensor(w1_s[:, bass.ds(e * W1C + 2 * H, 2 * H)],
                                         w1_st[:, :, :].rearrange("p a n -> p (a n)"), WSCALE,
                                         w1_s[:, bass.ds(e * W1C, 2 * H)], ALU.mult, ALU.subtract).then_inc(s_e_l1, 1)
                dve.wait_ge(s_e_h2, e + 1)
                dve.scalar_tensor_tensor(w2_s[:, bass.ds(e * W2C + HM * D, HM * D)], w2_st[:, :], WSCALE,
                                         w2_s[:, bass.ds(e * W2C, HM * D)], ALU.mult, ALU.subtract).then_inc(s_e_l2, 1)

            def state(b, k):
                dve.wait_ge(s_s_full, 7 * b + k + 1)
                ge(dve, s_sl_ok, 7 * b + k)
                if k == 0:
                    dve.tensor_copy(s32[:, :, :], ps_s[:, :, 0:D]).then_inc(s_s32_ok, 1)
                else:
                    dve.scalar_tensor_tensor(s32[:, :, :], s32[:, :, :], A128, ps_s[:, :, 0:D],
                                             ALU.mult, ALU.add).then_inc(s_s32_ok, 1)

            def best_two(g, u):
                dve.wait_ge(s_lg_full, g + 1)
                dve.tensor_copy(lg[:, :, :], ps_lg).then_inc(s_lg_ok, 1)
                dve.wait_ge(s_lg_ok, g + 1)
                settle(dve)
                for c in range(CH):
                    dve.max(top[:, c, :], lg[:, c, :]).then_inc(s_top_ok, 1)
                for c in range(CH):
                    dve.wait_ge(s_top_ok, CH * g + c + 1)
                    settle(dve)
                    dve.max_index(topi[:, c, :], top[:, c, :], lg[:, c, :]).then_inc(s_topi_ok, 1)
                dve.tensor_tensor(gap[:, :], top[:, :, 1], top[:, :, 0], ALU.subtract).then_inc(s_gap_ok, 1)
                dve.wait_ge(s_topi_ok, CH * g + CH)
                dve.tensor_copy(topf[:, :, :], topi[:, :, 0:2].rearrange("p c k -> p k c")).then_inc(s_topf_ok, 1)
                dve.wait_ge(s_topf_ok, g + 1)
                for k in range(K):
                    dve.tensor_tensor(hot[:, k, :, :], topf[:, k, :].unsqueeze(2).to_broadcast([P, CH, E]),
                                      cst[:, C_EX:C_EX + E].unsqueeze(1).to_broadcast([P, CH, E]), ALU.is_equal)\
                        .then_inc(s_hot_ok, 1)
                dve.wait_ge(s_hot_ok, 2 * g + 2)
                dve.tensor_tensor(hot16[:, :, :], hot[:, 0, :, :], hot[:, 1, :, :], ALU.add).then_inc(s_hot16_ok, 1)
                dve.tensor_tensor(assigned[:, bass.ds(g * CH * E, CH * E)], hot[:, 0, :, :].rearrange("p c e -> p (c e)"),
                                  hot[:, 1, :, :].rearrange("p c e -> p (c e)"), ALU.add).then_inc(s_hot16_ok, 1)

            def places(g, u, b):
                dve.wait_ge(s_egap_ok, g + 1)
                dve.tensor_scalar(egap1[:, :], egap[:, :], 1.0, None, ALU.add).then_inc(s_eg1_ok, 1)
                dve.wait_ge(s_eg1_ok, g + 1)
                settle(dve)
                dve.reciprocal(prio[:, bass.ds(g * CH, CH)], egap1[:, :]).then_inc(s_wt_ok, 1)
                dve.wait_ge(s_wt_ok, 5 * g + 1)
                dve.wait_ge(slot_st[u], 16 * K * CH * b + FREE)
                settle(dve)
                dve.tensor_copy(x2f[u][:, :, MF + 1], prio[:, bass.ds(g * CH, CH)]).then_inc(s_wt_ok, 1)
                dve.tensor_tensor(x2f[u][:, :, MF + 2], egap[:, :], prio[:, bass.ds(g * CH, CH)], ALU.mult)\
                    .then_inc(s_wt_ok, 1)
                dve.tensor_copy(x2f[u][:, :, MF + 3], topf[:, 0, :]).then_inc(s_wt_ok, 1)
                dve.tensor_copy(x2i[u][:, :, MF], tok_i[:, bass.ds(g * CH, CH)]).then_inc(s_wt_ok, 1)
                dve.wait_ge(s_pl_full, g + 1)
                dve.tensor_tensor(place[:, :, :], ps_pl, cst[:, C_REG:C_REG + E].unsqueeze(1).to_broadcast([P, CH, E]),
                                  ALU.add).then_inc(s_place_ok, 1)
                dve.tensor_reduce(hotred[:, :], hot16[:, :, :].rearrange("p c e -> p e c"), AX.X, ALU.add)\
                    .then_inc(s_hred_ok, 1)
                dve.wait_ge(s_place_ok, g + 1)
                for k in range(K):
                    dve.tensor_tensor(placed[:, k, :, :], hot[:, k, :, :], place[:, :, :], ALU.mult)\
                        .then_inc(s_placed_ok, 1)
                dve.wait_ge(s_hred_ok, g + 1)
                dve.tensor_tensor(hotsum[:, :], hotsum[:, :], hotred[:, :], ALU.add).then_inc(s_hsum_ok, 1)
                dve.wait_ge(s_placed_ok, 2 * g + 2)
                dve.tensor_reduce(slotf[:, :, :], placed[:, :, :, :], AX.X, ALU.add).then_inc(s_slotf_ok, 1)
                dve.wait_ge(s_hsum_ok, g + 1)
                dve.tensor_copy(hotsum16[:, :], hotsum[:, :]).then_inc(s_hs16_ok, 1)
                dve.wait_ge(s_slotf_ok, g + 1)
                dve.tensor_copy(slot[u][:, :, :], slotf[:, :, :]).then_inc(s_slot_ok, 1)

            def step(g, u, b, rows, attend, route, expert):
                v = 1 - u
                if route:
                    statistics(g - 1, 1, h2[v])
                    normalise(g - 1, 1, h2[v], x2n)
                if attend:
                    for a in range(2):
                        dve.wait_ge(s_qh_ok, 2 * g + a + 1)
                        dve.scalar_tensor_tensor(qs[:, 2 + a, :], ps_q[:, a, :], 1.0 / WSCALE, qs[:, a, :],
                                                 ALU.mult, ALU.subtract).then_inc(s_ql_ok, 1)
                    state(b, 4 * u)
                if route:
                    dve.wait_ge(s_x2h_ok, g)
                    dve.tensor_tensor(x2s[v][:, :, 2 * P:3 * P], x2n[:, :, 0:P], x2s[v][:, :, 0:P], ALU.subtract)\
                        .then_inc(s_x2l_ok, 1)
                    dve.tensor_tensor(x2s[v][:, :, D:D + D1 - 1], x2n[:, :, P:D - 1], x2s[v][:, :, P:D - 1],
                                      ALU.subtract).then_inc(s_x2l_ok, 1)
                if attend:
                    state(b, 4 * u + 1)
                    for a in range(2):
                        dve.wait_ge(s_p_full, g + 1)
                        dve.tensor_tensor(pt[:, 2 * a:2 * a + 2, :], ps_p[:, 2 * a:2 * a + 2, :],
                                          tri.unsqueeze(1).to_broadcast([P, 2, P]), ALU.mult).then_inc(s_pt_ok, 1)
                    state(b, 4 * u + 2)
                    for a in range(2):
                        dve.wait_ge(s_ph_ok, 2 * g + a + 1)
                        dve.tensor_tensor(ps[:, 1, 2 * a:2 * a + 2, :], pt[:, 2 * a:2 * a + 2, :],
                                          ps[:, 0, 2 * a:2 * a + 2, :], ALU.subtract).then_inc(s_pl_ok, 1)
                if route:
                    best_two(g - 1, v)
                if rows:
                    dve.wait_ge(h_ld[v], 16 * CH * (b + u) + 16 * CH)
                    statistics(g + 1, 0, h[v])
                if attend and u == 0:
                    state(b, 3)
                if expert is not None:
                    experts(expert)
                if rows:
                    normalise(g + 1, 0, h[v], xn[v])
                if route:
                    places(g - 1, v, b - 1 + u)
                if attend:
                    for a in range(2):
                        dve.wait_ge(s_zh_ok, 2 * g + a + 1)
                        dve.tensor_tensor(zs[:, 2:4, 2 * a * P:2 * (a + 1) * P], ps_z[a],
                                          zs[:, 0:2, 2 * a * P:2 * (a + 1) * P], ALU.subtract).then_inc(s_zl_ok, 1)
                    dve.wait_ge(out_st[u], 16 * b + FREE)
                    for c in range(CH):
                        if c % 2 == 0:
                            dve.wait_ge(s_a_full, 2 * g + c // 2 + 1)
                        dve.scalar_tensor_tensor(h2[u][:, c, :], ps_y[c // 2][:, c % 2, 0:D], out_scale, h[u][:, c, :],
                                                 ALU.mult, ALU.add).then_inc(s_h2_ok, 1)
                    dve.wait_ge(s_h2_ok, CH * g + CH)
                if expert is not None:
                    experts_low(expert)

            pipeline(dve, step)

            done = [0]

            def link(ins):
                done[0] += 1
                ins.then_inc(s_n_ok, 1)
                dve.wait_ge(s_n_ok, done[0])

            def by_tile(ap):
                return ap.unsqueeze(1).to_broadcast([P, NTAB, E])

            def by_expert(ap):
                return ap.unsqueeze(2).to_broadcast([P, NTAB, E])

            tab_n = cst[:, C_TAB:C_TAB + NTAB]
            dve.wait_ge(s_n_full, 1)
            link(dve.tensor_copy(cnt[:, :], ps_n))
            link(dve.tensor_tensor(padf[:, :], cnt[:, :], cst[:, C_REG:C_REG + E], ALU.add))
            dve.tensor_copy(pad_i[:, :], padf[:, :]).then_inc(s_pad_ok, 1)
            link(dve.tensor_reduce(over[:, 0:1], cnt[:, :], AX.X, ALU.max))
            link(dve.tensor_scalar(over[:, 1:2], over[:, 0:1], float(CAP), None, ALU.is_gt))
            link(dve.tensor_copy(over_i[:, :], over[:, 1:2]))
            dve.sem_inc(s_over_ok, 1)
            link(dve.memset(limit[:, :], 0.0))
            link(dve.memset(limit_tok[:, :], 0.0))
            link(dve.tensor_scalar(tiles_i[:, :], cnt[:, :], TM / 2 - 0.75, 1.0 / TM, ALU.add, ALU.mult))
            link(dve.tensor_copy(tiles_f[:, :], tiles_i[:, :]))
            link(dve.tensor_tensor_scan(ends[:, :], ones[:, 0:E], tiles_f[:, :], 0.0, ALU.mult, ALU.add))
            link(dve.tensor_tensor(past[:, :, :], by_expert(tab_n), by_tile(ends[:, :]), ALU.is_ge))
            link(dve.tensor_reduce(tab_e[:, :], past[:, :, :], AX.X, ALU.add))
            link(dve.tensor_tensor(prod[:, :, :], past[:, :, :], by_tile(tiles_f[:, :]), ALU.mult))
            link(dve.tensor_reduce(tab_start[:, :], prod[:, :, :], AX.X, ALU.add))
            link(dve.tensor_tensor(tab_off[:, :], tab_n, tab_start[:, :], ALU.subtract))
            link(dve.tensor_scalar(tab_row0[:, :], tab_e[:, :], float(E) - 0.5, float(TM), ALU.is_lt, ALU.mult))
            link(dve.tensor_tensor(tab_offv[:, :], tab_off[:, :], tab_row0[:, :], ALU.mult))
            link(dve.scalar_tensor_tensor(tab_row[:, :], tab_e[:, :], float(REGION), tab_offv[:, :], ALU.mult, ALU.add))
            link(dve.tensor_copy(tab_row_i[:, :], tab_row[:, :]))
            link(dve.tensor_scalar(tab_ew[:, :], tab_e[:, :], float(E - 1), None, ALU.min))
            link(dve.tensor_copy(tab_e_i[:, :], tab_ew[:, :]))
            dve.sem_inc(s_m_ok, 1)

            too_many = dve.value_load(over_i[0:1, 0:1], min_val=0, max_val=1)
            with dve.If(too_many != 0):
                def by_chunk(ap):
                    return ap.unsqueeze(2).to_broadcast([P, E, NCH])

                n0 = [0]

                def order(ins):
                    n0[0] += 1
                    ins.then_inc(s_b_ok, 1)
                    dve.wait_ge(s_b_ok, n0[0])

                order(dve.tensor_tensor(pm[:, :, :], assigned[:, :].rearrange("p (c e) -> p e c", e=E),
                                        prio[:, :].unsqueeze(1).to_broadcast([P, E, NCH]), ALU.mult))
                order(dve.memset(limit[:, :], 0.5))
                order(dve.memset(move[:, 0:1], 0.5))
                base = n0[0]
                NP = 24
                with dve.Fori(0, NP) as r:
                    STEPS = 7
                    at = base + r * STEPS
                    dve.tensor_scalar(cand[:, :], limit[:, :], move[:, 0:1], None, ALU.add).then_inc(s_b_ok, 1)
                    dve.wait_ge(s_b_ok, at + 1)
                    dve.tensor_tensor(cmp[:, :, :], pm[:, :, :], by_chunk(cand[:, :]), ALU.is_ge).then_inc(s_b_ok, 1)
                    dve.wait_ge(s_b_ok, at + 2)
                    dve.tensor_reduce(part_cnt[:, :], cmp[:, :, :], AX.X, ALU.add).then_inc(s_b_part, 1)
                    dve.wait_ge(s_b_tot, r + 1)
                    dve.tensor_scalar(took[:, :], ps_n, float(CAP), None, ALU.is_ge).then_inc(s_b_ok, 1)
                    dve.wait_ge(s_b_ok, at + 3)
                    dve.tensor_scalar(cand[:, :], took[:, :], move[:, 0:1], None, ALU.mult).then_inc(s_b_ok, 1)
                    dve.wait_ge(s_b_ok, at + 4)
                    dve.tensor_tensor(limit[:, :], limit[:, :], cand[:, :], ALU.add).then_inc(s_b_ok, 1)
                    dve.tensor_scalar(move[:, 1:2], move[:, 0:1], 0.5, None, ALU.mult).then_inc(s_b_ok, 1)
                    dve.wait_ge(s_b_ok, at + 6)
                    dve.tensor_copy(move[:, 0:1], move[:, 1:2]).then_inc(s_b_ok, 1)
                    dve.wait_ge(s_b_ok, at + 7)
                n0[0] = base + NP * 7
                order(dve.tensor_tensor(cmp[:, :, :], pm[:, :, :], by_chunk(limit[:, :]), ALU.is_gt))
                dve.tensor_reduce(part_cnt[:, :], cmp[:, :, :], AX.X, ALU.add).then_inc(s_b_part, 1)
                dve.wait_ge(s_b_tot, NP + 1)
                order(dve.tensor_scalar(room[:, :], ps_n, -1.0, float(CAP), ALU.mult, ALU.add))
                order(dve.tensor_tensor(tie[:, :, :], pm[:, :, :], by_chunk(limit[:, :]), ALU.is_equal))
                order(dve.memset(move[:, 0:1], float(T)))
                base = n0[0]
                NK = T.bit_length()
                with dve.Fori(0, NK) as r:
                    at = base + r * 8
                    dve.tensor_scalar(cand[:, :], limit_tok[:, :], move[:, 0:1], None, ALU.add).then_inc(s_b_ok, 1)
                    dve.wait_ge(s_b_ok, at + 1)
                    dve.tensor_tensor(cmp[:, :, :], cst[:, C_TOK:C_TOK + NCH].unsqueeze(1).to_broadcast([P, E, NCH]),
                                      by_chunk(cand[:, :]), ALU.is_lt).then_inc(s_b_ok, 1)
                    dve.wait_ge(s_b_ok, at + 2)
                    dve.tensor_tensor(cmp[:, :, :], cmp[:, :, :], tie[:, :, :], ALU.mult).then_inc(s_b_ok, 1)
                    dve.wait_ge(s_b_ok, at + 3)
                    dve.tensor_reduce(part_cnt[:, :], cmp[:, :, :], AX.X, ALU.add).then_inc(s_b_part, 1)
                    dve.wait_ge(s_b_tot, NP + 2 + r)
                    dve.tensor_tensor(took[:, :], ps_n, room[:, :], ALU.is_le).then_inc(s_b_ok, 1)
                    dve.wait_ge(s_b_ok, at + 4)
                    dve.tensor_scalar(cand[:, :], took[:, :], move[:, 0:1], None, ALU.mult).then_inc(s_b_ok, 1)
                    dve.wait_ge(s_b_ok, at + 5)
                    dve.tensor_tensor(limit_tok[:, :], limit_tok[:, :], cand[:, :], ALU.add).then_inc(s_b_ok, 1)
                    dve.tensor_scalar(move[:, 1:2], move[:, 0:1], 0.5, None, ALU.mult).then_inc(s_b_ok, 1)
                    dve.wait_ge(s_b_ok, at + 7)
                    dve.tensor_copy(move[:, 0:1], move[:, 1:2]).then_inc(s_b_ok, 1)
                    dve.wait_ge(s_b_ok, at + 8)

            for u in range(2):
                dve.wait_ge(out_st[u], 16 * B + FREE)
            link(dve.tensor_tensor(past[:, :, :], by_expert(tab_e[:, :]), by_tile(cst[:, C_EX:C_EX + E]), ALU.is_equal))
            link(dve.tensor_tensor(prod[:, :, :], past[:, :, :], by_tile(limit[:, :]), ALU.mult))
            link(dve.tensor_reduce(tab[:, :, 1], prod[:, :, :], AX.X, ALU.add))
            link(dve.tensor_tensor(prod[:, :, :], past[:, :, :], by_tile(limit_tok[:, :]), ALU.mult))
            link(dve.tensor_reduce(tab[:, :, 2], prod[:, :, :], AX.X, ALU.add))
            link(dve.tensor_copy(tab[:, :, 0], tab_e[:, :]))
            link(dve.tensor_copy(tab[:, :, 3], tab_e[:, :]))
            dve.sem_inc(s_t_w, 2)
            dve.sem_inc(s_t_osum, 2)
            dve.sem_inc(s_t_oy, 4)
            dve.wait_ge(s_b2_ld, 16 * E)

            def rows_in(j):
                dve.wait_ge(s_t_tp, j + 3)
                dve.tensor_copy(xtt[:, :, :], tview).then_inc(s_t_x, 1)

            rows_in(0)
            with dve.Fori(0, NT // 2) as i:
                for u in range(2):
                    j = 2 * i + u
                    for m in range(HB):
                        dve.wait_ge(s_t_gelu, HB * j + m + 1)
                        dve.wait_ge(s_t_hh, HB * j + m + 1 + HB)
                        dve.tensor_tensor(hs[:, 1, 2 * m:2 * m + 2, :], h32[:, 2 * m:2 * m + 2, :],
                                          hs[:, 0, 2 * m:2 * m + 2, :], ALU.subtract).then_inc(s_t_hl, 1)
                        if m == 0:
                            rows_in(j + 1)
                    dve.wait_ge(row_ld[u], 16 * i + 16)
                    dve.wait_ge(s_t_oy, 2 * j + 2)
                    dve.wait_ge(out_add, 32 * (j - 1) + ADD_FREE)
                    settle(dve)
                    w0, w1_, e0 = xrf[u][:, :, MF + 1], xrf[u][:, :, MF + 2], xrf[u][:, :, MF + 3]
                    dve.tensor_copy(tinfo[:, :], tab[:, bass.ds(j, 1), :].rearrange("p a b -> p (a b)"))\
                        .then_inc(s_t_info, 1)
                    dve.tensor_copy(wk[:, 0, :], xru[u][:, :, MF]).then_inc(s_t_info, 1)
                    dve.tensor_tensor(wk[:, 1, :], w0, w1_, ALU.subtract).then_inc(s_t_info, 1)
                    dve.tensor_copy(dest[u][:, :], xru[u][:, :, MF]).then_inc(s_t_info, 1)
                    dve.wait_ge(s_t_info, 9 * j + 3)
                    dve.scalar_tensor_tensor(wk[:, 2, :], e0, tinfo[:, 0:1], wk[:, 1, :], ALU.is_equal, ALU.mult)\
                        .then_inc(s_t_info, 1)
                    dve.tensor_scalar(wk[:, 3, :], wk[:, 0, :], tinfo[:, 2:3], None, ALU.is_lt).then_inc(s_t_info, 1)
                    dve.wait_ge(s_t_info, 9 * j + 6)
                    dve.tensor_tensor(wk[:, 4, :], wk[:, 2, :], w1_, ALU.add).then_inc(s_t_info, 1)
                    dve.scalar_tensor_tensor(wk[:, 5, :], w0, tinfo[:, 1:2], wk[:, 3, :], ALU.is_equal, ALU.mult)\
                        .then_inc(s_t_info, 1)
                    dve.wait_ge(s_t_info, 9 * j + 8)
                    dve.scalar_tensor_tensor(wk[:, 6, :], w0, tinfo[:, 1:2], wk[:, 5, :], ALU.is_gt, ALU.add)\
                        .then_inc(s_t_info, 1)
                    dve.wait_ge(s_t_info, 9 * j + 9)
                    dve.tensor_tensor(wfin[u][:, :], wk[:, 4, :], wk[:, 6, :], ALU.mult).then_inc(s_t_w, 1)
                    e = dve.value_load(tab_e_i[0:1, bass.ds(j, 1)], min_val=0, max_val=E - 1)
                    for b in range(2):
                        dve.wait_ge(s_t_o, j + 1)
                        dve.scalar_tensor_tensor(osum[u][:, b, :], ps_o[b], 1.0 / WSCALE, b2_s[:, bass.ds(e * D, D)],
                                                 ALU.mult, ALU.add).then_inc(s_t_osum, 1)

        @block.tensor
        def _(pe):
            pe.wait_ge(s_c_ld, 16)
            pe.wait_ge(s_xf_ok, 1)
            pe.transpose(ps_g[:, 0:NCH], x_rowsf[:, :], ident[0:NCH, 0:NCH]).then_inc(s_xtr_full, 1)

            def step(g, u, b, rows, attend, route, expert):
                v = 1 - u

                def turn(src, full):
                    for a in range(3):
                        for c in range(CH):
                            last = pe.transpose(ps_t[:, a, c * P:(c + 1) * P], src[:, c, a * P:(a + 1) * P], ident16[:, :])
                    last.then_inc(full, 1)

                def state(k):
                    c = k % CH
                    ge(pe, s_s32_ok, 7 * b + k)
                    for q, (l, r) in enumerate(((0, 0), (2, 0), (0, 1))):
                        lhs = xs[u][:, c, l * P:(l + 1) * P]
                        if r == 0:
                            pe.matmul(ps_s[:, 0, 0:D], lhs, xs[u][:, c, 0:D], start=(q == 0), stop=False)
                        else:
                            pe.matmul(ps_s[:, 0, 0:P], lhs, xs[u][:, c, 2 * P:3 * P], start=False, stop=False)
                            pe.matmul(ps_s[:, 0, P:D], lhs, xs[u][:, c, D:2 * P], start=False, stop=True)
                    lhs = xs[u][:, c, P:2 * P]
                    pe.matmul(ps_s[:, 1, 0:D], lhs, xs[u][:, c, 0:D], start=True, stop=False)
                    pe.matmul(ps_s[:, 1, 0:P], lhs, xs[u][:, c, 2 * P:3 * P], start=False, stop=False)
                    pe.matmul(ps_s[:, 1, P:D], lhs, xs[u][:, c, D:2 * P], start=False, stop=True).then_inc(s_s_full, 1)

                def products(c):
                    for n, (q, r) in enumerate(PASSES):
                        last = pe.matmul(ps_p[:, c, :], xt[u][:, r, c * P:(c + 1) * P], qs[:, q, c * P:(c + 1) * P],
                                         start=(n == 0), stop=(n == 4))
                    if c == CH - 1:
                        last.then_inc(s_p_full, 1)

                def sums(c):
                    k = 4 * u + c
                    ge(pe, s_pl_ok, 2 * g + c // 2 + 1)
                    if k > 0:
                        pe.wait_ge(s_sl_ok, 7 * b + k)
                    for a in range(2):
                        ops = [(xs[u][:, c, 0:P], ps[:, 0, c, :]), (xs[u][:, c, 2 * P:3 * P], ps[:, 0, c, :]),
                               (xs[u][:, c, 0:P], ps[:, 1, c, :])] if a == 0 else \
                              [(xs[u][:, c, P:2 * P], ps[:, 0, c, :]), (xs[u][:, c, P:2 * P], ps[:, 1, c, :])]
                        if k > 0:
                            ops += [(ss[(k - 1) % CH][:, l, a * P:(a + 1) * P], qs[:, q, c * P:(c + 1) * P])
                                    for l, q in PASSES6]
                        for n, (l, r) in enumerate(ops):
                            last = pe.matmul(ps_z[c // 2][:, a, (c % 2) * P:(c % 2 + 1) * P], l, r, start=(n == 0), stop=(n == len(ops) - 1))
                    last.then_inc(s_z_done, 1)

                def output(c):
                    if c % 2 == 0:
                        pe.wait_ge(s_zl_ok, 2 * g + c // 2 + 1)
                        ge(pe, s_h2_ok, CH * g)
                    for n, (w, z) in enumerate(PASSES6):
                        last = pe.matmul(ps_y[c // 2][:, c % 2, 0:D], zs[:, z, c * P:(c + 1) * P], v_s[:, w, :],
                                         start=(n == 0), stop=(n == 5))
                    if c % 2:
                        last.then_inc(s_a_full, 1)

                if attend:
                    pe.wait_ge(s_tp_a, g + 1)
                    ge(pe, s_zl_ok, 2 * g)
                    for a in range(2):
                        for n, (w, r) in enumerate(PASSES):
                            last = pe.matmul(ps_q[:, a, :], a_s[:, w, a * P:(a + 1) * P], xt[u][:, r, :],
                                             start=(n == 0), stop=(n == 4))
                        last.then_inc(s_q_full, 1)
                    state(4 * u)
                if route:
                    pe.wait_ge(s_x2l_ok, 2 * g)
                    if attend:
                        pe.wait_ge(s_tp_a, g + 1)
                    turn(x2s[v], s_tp2_full)
                if attend:
                    state(4 * u + 1)
                    pe.wait_ge(s_ql_ok, 2 * g + 2)
                    ge(pe, s_h2_ok, CH * g)
                    for c in range(CH):
                        products(c)
                    state(4 * u + 2)
                if route:
                    pe.wait_ge(s_tp2_a, g)
                    for c in range(CH):
                        for n, (w, r) in enumerate(PASSES):
                            last = pe.matmul(ps_lg[:, c, :], x2t[:, r, c * P:(c + 1) * P], g_s[:, w, :],
                                             start=(n == 0), stop=(n == 4))
                    last.then_inc(s_lg_full, 1)
                if attend:
                    sums(0)
                    sums(1)
                    if u == 0:
                        state(3)
                if route:
                    pe.wait_ge(s_hot16_ok, 2 * g)
                    for c in range(CH):
                        ops = [(ones16[:, :], hotsum16[:, :])] + [(ones16[:, :], hot16[:, a, :]) for a in range(c)] + \
                              [(upper16[:, :], hot16[:, c, :])]
                        for n, (l, r) in enumerate(ops):
                            last = pe.matmul(ps_pl[:, c, :], l, r, start=(n == 0), stop=(n == len(ops) - 1))
                    last.then_inc(s_pl_full, 1)
                if attend:
                    sums(2)
                    sums(3)
                    output(0)
                    output(1)
                if rows:
                    pe.wait_ge(s_xl_ok, 2 * g + 4)
                    ge(pe, s_tp2_a, g)
                    turn(xs[v], s_tp_full)
                if attend:
                    output(2)
                    output(3)

            def attention_weights():
                pe.wait_ge(s_w_bias, 32)
                for t in range(2):
                    for m in range(2):
                        rm, c0 = (P, D1)[m], t * D + m * P
                        pe.transpose(ps_q[0:rm, t, m * 2 * P:m * 2 * P + P], wst[:, 0, c0:c0 + rm], ident)
                        last = pe.transpose(ps_q[0:rm, t, m * 2 * P + P:m * 2 * P + D], wst[0:D1, 1, c0:c0 + rm],
                                            ident[0:D1, 0:D1])
                last.then_inc(s_w_tr, 1)
                pe.wait_ge(s_w_trc, 8)
                for b in range(2):
                    pe.matmul(ps_q[:, b, 0:2 * P], wqk_t[:, 0, 0, b * P:(b + 1) * P], wqk_t[:, 1, 0, :],
                              start=True, stop=False)
                    last = pe.matmul(ps_q[:, b, 0:2 * P], wqk_t[0:D1, 0, 1, b * P:(b + 1) * P], wqk_t[0:D1, 1, 1, :],
                                     start=False, stop=True)
                last.then_inc(s_w_a, 1)
                pe.wait_ge(s_v_l, 1)
                pe.wait_ge(s_w_al, 1)
                pe.wait_ge(s_g_l, 1)

            attention_weights()
            pe.wait_ge(s_c_16, 3)
            pe.wait_ge(s_c_init, 3 + 2 * (CH + 2) + CH + 4)
            pipeline(pe, step)

            pe.wait_ge(s_hs16_ok, 2 * B)
            pe.matmul(ps_n, ones16[:, :], hotsum16[:, :], start=True, stop=True).then_inc(s_n_full, 1)
            pe.wait_ge(s_over_ok, 1)
            too_many = pe.value_load(over_i[0:1, 0:1], min_val=0, max_val=1)
            with pe.If(too_many != 0):
                with pe.Fori(0, 24 + 1 + T.bit_length()) as r:
                    pe.wait_ge(s_b_part, r + 1)
                    pe.matmul(ps_n, ones, part_cnt[:, :], start=True, stop=True).then_inc(s_b_tot, 1)

            def turn(i, u):
                pe.wait_ge(row_ld[u], 16 * i + 16)
                for a in range(3):
                    for c in range(2):
                        last = pe.transpose(tview[:, a, c * P:(c + 1) * P], xrow[u][:, c, a * P:(a + 1) * P], ident16[:, :])
                last.then_inc(s_t_tp, 1)

            pe.wait_ge(s_m_ok, 1)
            pe.wait_ge(s_e_l1, E)
            pe.wait_ge(s_e_l2, E)
            pe.sem_inc(s_t_tp, 2)
            pe.sem_inc(s_t_hh, HB)
            pe.wait_ge(s_tp2_a, 2 * B)
            turn(0, 0)
            with pe.Fori(0, NT // 2) as i:
                for u in range(2):
                    j = 2 * i + u
                    e = pe.value_load(tab_e_i[0:1, bass.ds(j, 1)], min_val=0, max_val=E - 1)
                    pe.wait_ge(s_t_x, j + 1)
                    for m in range(HM):
                        if m % 2 == 0:
                            pe.wait_ge(s_t_hh, HB * j + m // 2 + 1)
                        for n, (a, r) in enumerate(PASSES):
                            last = pe.matmul(ps_h[m // 2][:, (m % 2) * TM:(m % 2 + 1) * TM],
                                             w1_s[:, bass.ds(e * W1C + a * H + m * P, P)], xtt[:, r, :],
                                             start=(n == 0), stop=(n == 4))
                        if m % 2:
                            last.then_inc(s_t_h, 1)
                    turn(i + u, 1 - u)
                    pe.wait_ge(s_t_osum, 2 * j + 2)
                    for m in range(HM):
                        if m % 2 == 0:
                            pe.wait_ge(s_t_hl, HB * j + m // 2 + 1)
                        for b in range(2):
                            for n, (v, w) in enumerate(((0, 0), (1, 0), (0, 1))):
                                last = pe.matmul(ps_o[b], hs[:, v, m, b * P:(b + 1) * P],
                                                 w2_s[:, bass.ds(e * W2C + w * HM * D + m * D, D)],
                                                 start=(m == 0 and n == 0), stop=(m == HM - 1 and n == 2))
                    last.then_inc(s_t_o, 1)


def kernel(x, L0_tok_weight, L0_attn_W_qkv, L0_attn_b_qkv, L0_ffn_Wg, L0_ffn_W1, L0_ffn_b1, L0_ffn_W2, L0_ffn_b2):
    import concourse.bacc as bacc
    from concourse.bass_utils import run_bass_kernel_spmd

    nc = bacc.Bacc("TRN2", target_bir_lowering=False, num_devices=1)
    B, S = x.shape
    T, D, E = B * S, L0_tok_weight.shape[1], L0_ffn_Wg.shape[1]
    consts = constants(T, E, T + TM, T * 2 // TM + E + 2)
    arrays, args = {}, []
    for name, a in (("x", x), ("emb", L0_tok_weight), ("w_qkv", L0_attn_W_qkv), ("b_qkv", L0_attn_b_qkv),
                    ("wg", L0_ffn_Wg), ("w1", L0_ffn_W1), ("b1", L0_ffn_b1), ("w2", L0_ffn_W2), ("b2", L0_ffn_b2),
                    ("consts", consts)):
        a = np.ascontiguousarray(a)
        arrays["in_" + name] = a
        args.append(nc.dram_tensor("in_" + name, a.shape, mybir.dt.from_np(a.dtype), kind="ExternalInput").ap())
    out = nc.dram_tensor("out_0", (T + TM, D), F32, kind="ExternalOutput").ap()
    lm_tower(nc, *args, out)
    r = run_bass_kernel_spmd(nc, [arrays], core_ids=[0])
    return r.results[0]["out_0"][0:T].reshape(B, S, D)
```

```python
from contextlib import ExitStack

import numpy as np
import concourse.bass as bass
from concourse import mybir

ALU = mybir.AluOpType
ACT = mybir.ActivationFunctionType
F32 = mybir.dt.float32
F16 = mybir.dt.float16
I32 = mybir.dt.int32
U32 = mybir.dt.uint32
AX = mybir.AxisListType

P = 128
ALPHA = 0.99
LN_EPS = 1e-5
WSCALE = 64.0
CH = 4
GT = CH * P
TM = 256
META = 8
NCONST = 688

C_ID, C_UP, C_MASK, C_ONE, C_EX, C_REG, C_TOK, C_TAB, C_PAD = 0, 128, 256, 384, 512, 520, 528, 592, 672
C_ROW, C_VAR, C_OUT, C_POW = 674, 675, 676, 678


def constants(T, E, region, ntab):
    c = np.zeros((P, NCONST), np.float64)
    a = float(np.float32(ALPHA))
    s, t = np.arange(P)[:, None], np.arange(P)[None, :]
    c[:, C_ID:C_ID + P] = s == t
    c[:, C_UP:C_UP + P] = s < t
    c[:, C_MASK:C_MASK + P] = np.where(s <= t, a ** -P, 0.0)
    c[:, C_ONE:C_ONE + P] = 1.0
    p = np.arange(P, dtype=np.float64)
    c[:, C_ROW] = a ** (-p / 2)
    c[:, C_VAR] = a ** p
    c[:, C_OUT] = a ** (P + 1.5 * p) / WSCALE
    c[:, C_POW:C_POW + CH] = -0.5
    c[:, C_EX:C_EX + E] = np.arange(E)
    c[:, C_REG:C_REG + E] = np.arange(E) * region
    c[:, C_TOK:C_TOK + T // P] = np.arange(T // P)[None, :] * P + s
    c[:, C_TAB:C_TAB + ntab] = np.arange(ntab)
    c[:, C_PAD:C_PAD + 2] = T + np.arange(2)[None, :] * P + s
    return c.astype(np.float32)


def lm_tower(nc, x, emb, w_qkv, b_qkv, wg, w1, b1, w2, b2, consts, out):
    B, S = x.shape
    T = B * S
    D = emb.shape[1]
    E = wg.shape[1]
    H = w1.shape[2]
    K = 2
    NCH = T // P
    D1 = D - P
    HM = H // P
    HB = HM // 2
    CAP = int(1.25 * T * K / E)
    NT = T * K // TM + E
    SURE = T * K // TM
    NTAB = NT + 2
    REGION = T + TM
    ROW = 2 * D + META
    MF = D
    W1C, W2C = 4 * H, 2 * HM * D
    A128 = float(np.float64(np.float32(ALPHA)) ** P)
    assert S == 2 * GT and D1 == 64 and B == E and SURE % 4 == 0 and NT % 2 == 0 and T + TM == out.shape[0]

    disp = nc.dram_tensor("disp", [E * REGION + TM, ROW // 2], I32, kind="Internal").ap()

    with ExitStack() as ctx:
        def sem(name):
            return ctx.enter_context(nc.semaphore(name))

        def sb(name, shape, dt):
            return ctx.enter_context(nc.sbuf_tensor(name, shape, dt))

        def psum(name, shape, dt):
            return ctx.enter_context(nc.psum_tensor(name, shape, dt))

        ps_t = psum("ps_t", [P, 4, GT], F16)
        ps_q = psum("ps_q", [P, 2, GT], F32)
        ps_p = psum("ps_p", [P, CH, P], F32)
        ps_s = psum("ps_s", [P, 2, 2 * P], F32)
        ps_a = psum("ps_a", [P, 2, 2 * P], F32)
        ps_g = psum("ps_g", [P, 512], F32)
        ps_h = [ps_q[:, 0, :], ps_q[:, 1, :], ps_p[:, :, :].rearrange("p a b -> p (a b)")]
        ps_o = [ps_s[:, 0, 0:D], ps_a[:, 0, 0:D]]
        ps_z = [ps_q[:, n, :].rearrange("p (a t) -> p a t", a=2) for n in range(2)]
        ps_y = [ps_a, ps_p[:, :, :].rearrange("p (c a) t -> p c (a t)", c=2)]
        ps_lg = ps_g[:, 0:CH * E].rearrange("p (c e) -> p c e", e=E)
        ps_pl = ps_g[:, 64:64 + CH * E].rearrange("p (c e) -> p c e", e=E)
        ps_n = ps_g[:, 128:128 + E]

        cst = sb("cst", [P, NCONST], F32)
        ident = cst[:, C_ID:C_ID + P]
        ones = cst[:, C_ONE:C_ONE + P]
        tri = cst[:, C_MASK:C_MASK + P]
        row_scale = cst[:, C_ROW:C_ROW + 1]
        var_scale = cst[:, C_VAR:C_VAR + 1]
        out_scale = cst[:, C_OUT:C_OUT + 1]
        minus_half = cst[:, C_POW:C_POW + CH]
        ident16 = sb("ident16", [P, P], F16)
        upper16 = sb("upper16", [P, P], F16)
        ones16 = sb("ones16", [P, P], F16)
        tok_i = sb("tok_i", [P, NCH], I32)
        x_rows = sb("x_rows", [NCH, P], I32)
        x_rowsf = sb("x_rowsf", [NCH, P], F32)
        ids = sb("ids", [P, NCH], U32)

        wst = sb("wst", [P, 2, 3 * D], F32)
        wlast = sb("wlast", [P, 3 * D], F32)
        wqk_t = sb("wqk_t", [P, 2, 2, 2 * P], F32)
        a_s = sb("a_s", [P, 4, 2 * P], F16)
        v_s = sb("v_s", [P, 4, D], F16)
        g_st = sb("g_st", [P, 2, E], F32)
        g_last = sb("g_last", [P, E], F32)
        g_zero = sb("g_zero", [2, E], F32)
        g_s = sb("g_s", [P, 4, E], F16)

        w1_st = sb("w1_st", [P, 2, H], F32)
        w1_last = sb("w1_last", [P, H], F32)
        w2_st = sb("w2_st", [P, HM * D], F32)
        w1_s = sb("w1_s", [P, E * W1C], F16)
        w2_s = sb("w2_s", [P, E * W2C], F16)
        b2_s = sb("b2_s", [P, E * D], F32)

        idg = [sb(f"idg{u}", [P, CH], U32) for u in range(2)]
        hr = [sb(f"hr{w}", [P, CH, D], F32) for w in range(4)]
        xn = [sb(f"xn{u}", [P, CH, D], F32) for u in range(2)]
        xs = [sb(f"xs{u}", [P, CH, 2 * D], F16) for u in range(2)]
        xt = [sb(f"xt{u}", [P, 3, GT], F16) for u in range(2)]
        st = [sb(f"st{n}", [P, CH, 6], F32) for n in range(2)]
        mv = [sb(f"mv{n}", [P, CH, 2], F32) for n in range(2)]
        var = [sb(f"var{n}", [P, CH], F32) for n in range(2)]
        rstd = [sb(f"rstd{n}", [P, CH], F32) for n in range(2)]
        neg_mean = [sb(f"neg_mean{n}", [P, CH], F32) for n in range(2)]
        shift = [sb(f"shift{n}", [P, CH], F32) for n in range(2)]
        qzs = sb("qzs", [P, 8, GT], F16)
        qs, zs = qzs[:, 0:4, :], qzs[:, 4:8, :]
        pt = sb("pt", [P, CH, P], F32)
        ps = sb("ps", [P, 2, CH, P], F16)
        s32 = sb("s32", [P, 2, D], F32)
        ss = [sb(f"ss{c}", [P, 4, 2 * P], F16) for c in range(CH)]
        x2n = sb("x2n", [P, CH, D], F32)
        x2s = [sb(f"x2s{u}", [P, CH, ROW], F16) for u in range(2)]
        x2f = [x2s[u][:, :, :].rearrange("p c r -> p (c r)").bitcast(F32).rearrange("p (c r) -> p c r", c=CH) for u in range(2)]
        x2i = [x2s[u][:, :, :].rearrange("p c r -> p (c r)").bitcast(I32).rearrange("p (c r) -> p c r", c=CH) for u in range(2)]
        x2t = sb("x2t", [P, 3, GT], F16)
        lg = sb("lg", [P, CH, E], F32)
        top = sb("top", [P, CH, 8], F32)
        topi = sb("topi", [P, CH, 8], U32)
        topf = sb("topf", [P, 2, CH], F32)
        hot = sb("hot", [P, 2, CH, E], F32)
        hot16 = sb("hot16", [P, CH, E], F16)
        hotsum = sb("hotsum", [P, E], F32)
        hotred = sb("hotred", [P, E], F32)
        hotsum16 = sb("hotsum16", [P, E], F16)
        gap = sb("gap", [P, CH], F32)
        egap = sb("egap", [P, CH], F32)
        egap1 = sb("egap1", [P, CH], F32)
        place = sb("place", [P, CH, E], F32)
        placed = sb("placed", [P, 2, CH, E], F32)
        slotf = sb("slotf", [P, 2, CH], F32)
        slot = [sb(f"slot{u}", [P, 2, CH], U32) for u in range(2)]
        prio = sb("prio", [P, NCH], F32)
        assigned = sb("assigned", [P, NCH * E], F32)

        cnt = sb("cnt", [P, E], F32)
        padf = sb("padf", [P, E], F32)
        pad_i = sb("pad_i", [P, E], I32)
        tiles_i = sb("tiles_i", [P, E], I32)
        tiles_f = sb("tiles_f", [P, E], F32)
        ends = sb("ends", [P, E], F32)
        past = xn[1][:, :, :].rearrange("p a b -> p (a b)")[:, 0:NTAB * E].rearrange("p (a b) -> p a b", b=E)
        prod = x2n[:, :, :].rearrange("p a b -> p (a b)")[:, 0:NTAB * E].rearrange("p (a b) -> p a b", b=E)
        tab_e = sb("tab_e", [P, NTAB], F32)
        tab_ew = sb("tab_ew", [P, NTAB], F32)
        tab_start = sb("tab_start", [P, NTAB], F32)
        tab_off = sb("tab_off", [P, NTAB], F32)
        tab_offv = sb("tab_offv", [P, NTAB], F32)
        tab_row0 = sb("tab_row0", [P, NTAB], F32)
        tab_row = sb("tab_row", [P, NTAB], F32)
        tab_row_i = sb("tab_row_i", [P, NTAB], I32)
        tab_e_i = sb("tab_e_i", [P, NTAB], I32)
        live = sb("live", [P, (NT - SURE) // 2], F32)
        live_i = sb("live_i", [P, (NT - SURE) // 2], I32)
        tab = sb("tab", [P, NTAB, 4], F32)
        over = sb("over", [P, 2], F32)
        over_i = sb("over_i", [P, 1], I32)
        limit = sb("limit", [P, E], F32)
        limit_tok = sb("limit_tok", [P, E], F32)
        pm = xn[0][:, :, :].rearrange("p a b -> p (a b)")[:, 0:E * NCH].rearrange("p (a b) -> p a b", b=NCH)
        tie = xn[1][:, :, :].rearrange("p a b -> p (a b)")[:, 0:E * NCH].rearrange("p (a b) -> p a b", b=NCH)
        cmp = hr[2][:, :, :].rearrange("p a b -> p (a b)")[:, 0:E * NCH].rearrange("p (a b) -> p a b", b=NCH)
        part_cnt = sb("part_cnt", [P, E], F32)
        cand = sb("cand", [P, E], F32)
        took = sb("took", [P, E], F32)
        room = sb("room", [P, E], F32)
        move = sb("move", [P, 2], F32)
        pad_rows = sb("pad_rows", [P, 2, ROW], F16)
        pad_u = pad_rows[:, :, :].rearrange("p c r -> p (c r)").bitcast(I32).rearrange("p (c r) -> p c r", c=2)

        out_zero = x2n[:, 0:2, :]

        tview = ps_t[:, 0:2, :].rearrange("p a b -> p (a b)")[:, 0:3 * TM].rearrange("p (a b) -> p a b", b=TM)
        xrow = [sb(f"xrow{u}", [P, 2, ROW], F16) for u in range(2)]
        xrf = [xrow[u][:, :, :].rearrange("p c r -> p (c r)").bitcast(F32).rearrange("p (c r) -> p c r", c=2) for u in range(2)]
        xru = [xrow[u][:, :, :].rearrange("p c r -> p (c r)").bitcast(U32).rearrange("p (c r) -> p c r", c=2) for u in range(2)]
        xri = [xrow[u][:, :, :].rearrange("p c r -> p (c r)").bitcast(I32).rearrange("p (c r) -> p c r", c=2) for u in range(2)]
        xtt = x2t[:, :, 0:TM]
        h32 = w1_st[:, :, :].rearrange("p a b -> p (a b)").rearrange("p (a b) -> p a b", b=TM)
        hs = qzs[:, :, :].rearrange("p a b -> p (a b)")[:, 0:2 * HM * TM].rearrange("p (v m b) -> p v m b", v=2, b=TM)
        osum = [hr[u][:, 0:2, :] for u in range(2)]
        oy = [hr[u][:, 2:4, :] for u in range(2)]
        tinfo = sb("tinfo", [P, 4], F32)
        dest = [sb(f"dest{u}", [P, 2], U32) for u in range(2)]
        wk = sb("wk", [P, 7, 2], F32)
        wfin = [sb(f"wfin{u}", [P, 2], F32) for u in range(2)]

        s_c_ld = sem("c_ld")
        s_c_up = sem("c_up")
        s_c_16 = sem("c_16")
        s_c_init = sem("c_init")
        s_x_ld = sem("x_ld")
        s_xf_ok = sem("xf_ok")
        s_xtr_full = sem("xtr_full")
        s_ids_ok = sem("ids_ok")
        s_w_ld = sem("w_ld")
        s_w_sub = sem("w_sub")
        s_w_bias = sem("w_bias")
        s_w_tr = sem("w_tr")
        s_w_trc = sem("w_trc")
        s_w_a = sem("w_a")
        s_w_ah = sem("w_ah")
        s_w_al = sem("w_al")
        s_v_h = sem("v_h")
        s_v_l = sem("v_l")
        s_g_ld = sem("g_ld")
        s_g_z = sem("g_z")
        s_g_sub = sem("g_sub")
        s_g_bias = sem("g_bias")
        s_g_h = sem("g_h")
        s_g_l = sem("g_l")
        s_b2_ld = sem("b2_ld")
        s_idg_ok = sem("idg_ok")
        s_bn_ok = sem("bn_ok")
        s_mv_ok = sem("mv_ok")
        s_rstd_ok = sem("rstd_ok")
        s_xn_ok = sem("xn_ok")
        s_xh_ok = sem("xh_ok")
        s_xl_ok = sem("xl_ok")
        s_tp_full = sem("tp_full")
        s_tp_a = sem("tp_a")
        s_tp_d = sem("tp_d")
        s_q_full = sem("q_full")
        s_qh_ok = sem("qh_ok")
        s_ql_ok = sem("ql_ok")
        s_p_full = sem("p_full")
        s_pt_ok = sem("pt_ok")
        s_ph_ok = sem("ph_ok")
        s_pl_ok = sem("pl_ok")
        s_s_full = sem("s_full")
        s_s32_ok = sem("s32_ok")
        s_sh_ok = sem("sh_ok")
        s_sl_ok = sem("sl_ok")
        s_zh_ok = sem("zh_ok")
        s_zl_ok = sem("zl_ok")
        s_a_full = sem("a_full")
        s_h2_ok = sem("h2_ok")
        s_bn2_ok = sem("bn2_ok")
        s_mv2_ok = sem("mv2_ok")
        s_rstd2_ok = sem("rstd2_ok")
        s_x2n_ok = sem("x2n_ok")
        s_x2h_ok = sem("x2h_ok")
        s_x2l_ok = sem("x2l_ok")
        s_tp2_full = sem("tp2_full")
        s_tp2_a = sem("tp2_a")
        s_tp2_d = sem("tp2_d")
        s_lg_full = sem("lg_full")
        s_lg_ok = sem("lg_ok")
        s_top_ok = sem("top_ok")
        s_topi_ok = sem("topi_ok")
        s_topf_ok = sem("topf_ok")
        s_hot_ok = sem("hot_ok")
        s_hot16_ok = sem("hot16_ok")
        s_gap_ok = sem("gap_ok")
        s_egap_ok = sem("egap_ok")
        s_eg1_ok = sem("eg1_ok")
        s_wt_ok = sem("wt_ok")
        s_hred_ok = sem("hred_ok")
        s_hsum_ok = sem("hsum_ok")
        s_hs16_ok = sem("hs16_ok")
        s_pl_full = sem("pl_full")
        s_place_ok = sem("place_ok")
        s_placed_ok = sem("placed_ok")
        s_slotf_ok = sem("slotf_ok")
        s_slot_ok = sem("slot_ok")
        s_e_ld = sem("e_ld")
        s_e_sub = sem("e_sub")
        s_e_bias = sem("e_bias")
        s_e_h1 = sem("e_h1")
        s_e_l1 = sem("e_l1")
        s_e_h2 = sem("e_h2")
        s_e_l2 = sem("e_l2")
        s_pad_tok = sem("pad_tok")
        s_pad_st = sem("pad_st")
        s_n_full = sem("n_full")
        s_m_ok = sem("m_ok")
        s_pad_ok = sem("pad_ok")
        s_over_ok = sem("over_ok")
        s_b_part = sem("b_part")
        s_b_tot = sem("b_tot")
        s_b_ok = sem("b_ok")
        s_tab_ok = sem("tab_ok")
        s_t_x = sem("t_x")
        s_t_h = sem("t_h")
        s_t_gelu = sem("t_gelu")
        s_t_hh = sem("t_hh")
        s_t_hl = sem("t_hl")
        s_t_o = sem("t_o")
        s_t_osum = sem("t_osum")
        s_t_oy = sem("t_oy")
        s_t_info = sem("t_info")
        s_t_dest = sem("t_dest")
        s_settled = sem("settled")
        s_z_done = sem("z_done")
        s_z_pad = sem("z_pad")
        s_t_w = sem("t_w")
        s_t_tp = sem("t_tp")
        s_n_ok = sem("n_ok")
        s_var_ok = sem("var_ok")
        s_var2_ok = sem("var2_ok")
        s_shift_ok = sem("shift_ok")
        s_shift2_ok = sem("shift2_ok")
        h_ld = [ctx.enter_context(nc.semaphore(f"h_ld{w}")) for w in range(4)]
        out_st = [ctx.enter_context(nc.semaphore(f"out_st{w}")) for w in range(4)]
        slot_st = [ctx.enter_context(nc.semaphore(f"slot_st{u}")) for u in range(2)]
        row_ld = [ctx.enter_context(nc.semaphore(f"row_ld{u}")) for u in range(2)]
        out_add = ctx.enter_context(nc.semaphore("out_add"))
        pad_ld = ctx.enter_context(nc.semaphore("pad_ld"))

        PASSES = ((0, 0), (0, 2), (2, 0), (1, 1), (3, 1))
        PASSES6 = ((0, 0), (0, 2), (2, 0), (1, 1), (1, 3), (3, 1))

        def settle(eng):
            eng.sem_inc(s_settled, 1)

        block = ctx.enter_context(nc.Block())

        def ge(eng, semaphore, value):
            if isinstance(value, int) and value <= 0:
                return
            eng.wait_ge(semaphore, value)

        def pipeline(eng, step):
            step(0, -1, True, True, False, False, False)
            step(0, 0, True, True, True, False, False)
            step(0, 1, True, True, True, True, False)
            with eng.Fori(0, B // 2 - 1) as i:
                for c in range(2, 6):
                    step(i, c, True, True, True, True, True)
            step(0, 2 * B - 2, False, True, True, True, True)
            step(0, 2 * B - 1, False, False, True, True, True)
            step(0, 2 * B, False, False, False, True, True)
            step(0, 2 * B + 1, False, False, False, False, True)

        def over_tiles(eng, tile):
            with eng.Fori(0, SURE // 4) as i:
                for k in range(4):
                    tile(2 * i + k // 2, k % 2)
            with eng.Fori(0, (NT - SURE) // 2) as i:
                has_rows = eng.value_load(live_i[0:1, bass.ds(i, 1)], min_val=0, max_val=1)
                with eng.If(has_rows != 0):
                    for u in range(2):
                        tile(i + SURE // 2, u)

        ADD_FREE = 64
        FREE = 16

        @block.sync
        def _(sp):
            sp.dma_start(cst[:, :], consts).then_inc(s_c_ld, 16)
            sp.dma_start(x_rows[:, :], x.rearrange("b (r p) -> (b r) p", p=P)).then_inc(s_x_ld, 16)
            sp.dma_start(wst[:, 0, :], w_qkv[0:P, :]).then_inc(s_w_ld, 16)
            sp.dma_start(wst[0:D1, 1, :], w_qkv[P:D, :]).then_inc(s_w_ld, 16)
            sp.dma_start(wst[D1:P, 1, :], w_qkv[P:D, :]).then_inc(s_w_ld, 16)
            sp.dma_start(wlast[:, :], w_qkv[D - 1:D, :].to_broadcast([P, 3 * D])).then_inc(s_w_ld, 16)
            for w in range(4):
                sp.sem_inc(out_st[w], FREE)
            sp.wait_ge(s_w_sub, 2)
            for r in (D1 - 1, P - 1):
                sp.dma_start(wst[r:r + 1, 1, :], b_qkv.rearrange("(a n) -> a n", a=1)).then_inc(s_w_bias, 16)
            sp.dma_start(g_st[:, 0, :], wg[0:P, :]).then_inc(s_g_ld, 16)
            sp.dma_start(g_st[0:D1, 1, :], wg[P:D, :]).then_inc(s_g_ld, 16)
            sp.dma_start(g_st[D1:P, 1, :], wg[P:D, :]).then_inc(s_g_ld, 16)
            sp.dma_start(g_last[:, :], wg[D - 1:D, :].to_broadcast([P, E])).then_inc(s_g_ld, 16)
            sp.wait_ge(s_g_sub, 2)
            sp.wait_ge(s_g_z, 1)
            for r in (D1 - 1, P - 1):
                sp.dma_start(g_st[r:r + 1, 1, :], g_zero[0:1, :]).then_inc(s_g_bias, 16)
            for e in range(E):
                sp.dma_start(b2_s[:, e * D:(e + 1) * D], b2[e:e + 1, :].to_broadcast([P, D])).then_inc(s_b2_ld, 16)

            def step(i, n, fetch, rows, attend, route, late):
                g, u, b = 4 * i + n, n % 2, 2 * i + n // 2
                if attend and u == 0:
                    e = b
                    ge(sp, s_e_l1, 2 * e)
                    ge(sp, s_e_l2, e)
                    sp.dma_start(w1_st[:, 0, :], w1[bass.ds(e, 1), 0:P, :].rearrange("e p n -> (e p) n"))\
                        .then_inc(s_e_ld, 16)
                    sp.dma_start(w1_st[0:D1, 1, :], w1[bass.ds(e, 1), P:D, :].rearrange("e p n -> (e p) n"))\
                        .then_inc(s_e_ld, 16)
                    sp.dma_start(w1_st[D1:P, 1, :], w1[bass.ds(e, 1), P:D, :].rearrange("e p n -> (e p) n"))\
                        .then_inc(s_e_ld, 16)
                    sp.dma_start(w1_last[:, :], w1[bass.ds(e, 1), D - 1, :].to_broadcast([P, H])).then_inc(s_e_ld, 16)
                    sp.dma_start(w2_st[:, :].rearrange("p (m n) -> p m n", m=HM),
                                 w2[bass.ds(e, 1), :, :].rearrange("e (m p) n -> p (e m) n", p=P)).then_inc(s_e_ld, 16)
                    sp.wait_ge(s_e_sub, 2 * e + 2)
                    for r in (D1 - 1, P - 1):
                        sp.dma_start(w1_st[r:r + 1, 1, :], b1[bass.ds(e, 1), :]).then_inc(s_e_bias, 16)
                if attend:
                    sp.wait_ge(s_h2_ok, CH * g + CH)
                    sp.dma_start(out[bass.ds(g * GT, GT), :].rearrange("(c p) d -> p c d", p=P),
                                 hr[n % 4][:, :, :]).then_inc(out_st[n % 4], 16)

            pipeline(sp, step)

            sp.wait_ge(s_pad_ok, 1)
            for e in range(E):
                first = sp.value_load(pad_i[0:1, e:e + 1], min_val=e * REGION, max_val=e * REGION + T)
                sp.dma_start(disp[bass.ds(first, TM), :].rearrange("(h p) c -> p h c", p=P),
                             pad_u).then_inc(pad_ld, 16)
            sp.wait_ge(pad_ld, 16 * E)
            for u in range(2):
                sp.wait_ge(slot_st[u], 16 * K * CH * B + FREE)
            sp.wait_ge(s_m_ok, 1)

            def load(i, u):
                sp.wait_ge(s_t_tp, 2 * i + u + 1)
                sp.wait_ge(s_t_w, 2 * i + u + 1)
                first = sp.value_load(tab_row_i[0:1, bass.ds(2 * i + u, 1)], min_val=0, max_val=E * REGION)
                sp.dma_start(xri[u], disp[bass.ds(first, TM), :].rearrange("(h p) c -> p h c", p=P))\
                    .then_inc(row_ld[u], 16)

            with sp.Fori(0, SURE // 2 + 1) as i:
                for u in range(2):
                    load(i, u)
            with sp.Fori(0, (NT - SURE) // 2) as i:
                has_rows = sp.value_load(live_i[0:1, bass.ds(i, 1)], min_val=0, max_val=1)
                with sp.If(has_rows != 0):
                    for u in range(2):
                        load(i + SURE // 2 + 1, u)
                    for u in range(2):
                        sp.wait_ge(row_ld[u], 16 * (i + SURE // 2 + 2))
                    sp.wait_ge(out_add, 64 * (i + SURE // 2 + 1) + ADD_FREE)
                    settle(sp)
            for u in range(2):
                sp.wait_ge(row_ld[u], 16 * (SURE // 2 + 1))
            sp.wait_ge(out_add, 32 * SURE + ADD_FREE)

        @block.gpsimd
        def _(pool):
            def first_stores():
                pool.wait_ge(s_pad_tok, 1)
                pool.wait_ge(s_z_pad, 1)
                pool.wait_ge(s_c_ld, 16)
                pool.tensor_copy(pad_u[:, :, MF], cst[:, C_PAD:C_PAD + 2]).then_inc(s_pad_tok, 1)
                pool.wait_ge(s_pad_tok, 2)
                for u in range(2):
                    pool.dma_start(disp[E * REGION + u * P:E * REGION + (u + 1) * P, :], pad_u[:, u, :])\
                        .then_inc(slot_st[u], FREE)
                for q in range(ADD_FREE // 16):
                    pool.dma_start(out[T + q * D1:T + (q + 1) * D1, :], out_zero[0:D1, 0, :]).then_inc(out_add, 16)

            def gather(i, n):
                g, u, w, before = 4 * i + n, n % 2, n % 4, i + n // 4
                if n >= 2:
                    pool.wait_ge(h_ld[(n - 2) % 4], 16 * CH * (i + (n - 2) // 4 + 1))
                    settle(pool)
                pool.tensor_copy(idg[u][:, :], ids[:, bass.ds(g * CH, CH)]).then_inc(s_idg_ok, 1)
                pool.wait_ge(s_idg_ok, g + 1)
                ge(pool, s_x2n_ok, CH * (g - 3))
                pool.wait_ge(out_st[w], 16 * before + FREE)
                settle(pool)
                for c in range(CH):
                    pool.indirect_dma_start(hr[w][:, c, :], None, emb[:, :],
                                            bass.IndirectOffsetOnAxis(ap=idg[u][:, c:c + 1], axis=0))\
                        .then_inc(h_ld[w], 16)

            def deviation(g, n):
                mv_ok, var_ok, rstd_ok, shift_ok = ((s_mv_ok, s_var_ok, s_rstd_ok, s_shift_ok),
                                                    (s_mv2_ok, s_var2_ok, s_rstd2_ok, s_shift2_ok))[n]
                pool.wait_ge(mv_ok, CH * g + CH)
                settle(pool)
                pool.tensor_scalar(var[n][:, :], mv[n][:, :, 1], LN_EPS, (var_scale, 1.0)[n], ALU.add, ALU.mult)\
                    .then_inc(var_ok, 1)
                pool.tensor_scalar(neg_mean[n][:, :], mv[n][:, :, 0], -1.0, None, ALU.mult).then_inc(var_ok, 1)
                pool.wait_ge(var_ok, 2 * g + 2)
                pool.tensor_tensor(rstd[n][:, :], var[n][:, :], minus_half, ALU.pow).then_inc(rstd_ok, 1)
                pool.wait_ge(rstd_ok, g + 1)
                pool.tensor_tensor(shift[n][:, :], neg_mean[n][:, :], rstd[n][:, :], ALU.mult).then_inc(shift_ok, 1)

            def low_rows(g, u):
                pool.wait_ge(s_xh_ok, g + 1)
                pool.tensor_tensor(xs[u][:, :, 2 * P:3 * P], xn[u][:, :, 0:P], xs[u][:, :, 0:P], ALU.subtract)\
                    .then_inc(s_xl_ok, 1)
                pool.tensor_tensor(xs[u][:, :, D:D + D1 - 1], xn[u][:, :, P:D - 1], xs[u][:, :, P:D - 1],
                                   ALU.subtract).then_inc(s_xl_ok, 1)

            def scatter(u, k):
                for c in range(CH):
                    pool.indirect_dma_start(disp[:, :], bass.IndirectOffsetOnAxis(ap=slot[u][:, k, c:c + 1], axis=0),
                                            x2i[u][:, c, :], None).then_inc(slot_st[u], 16)

            def step(i, n, fetch, rows, attend, route, late):
                g, u, b = 4 * i + n, n % 2, 2 * i + n // 2
                v = 1 - u
                if n == 0:
                    first_stores()
                if rows:
                    low_rows(g + 1, v)
                if route:
                    deviation(g - 1, 1)
                if fetch and n >= 0:
                    gather(i, n + 2)
                if late:
                    pool.wait_ge(s_x2l_ok, 2 * (g - 1))
                    pool.wait_ge(s_wt_ok, 5 * (g - 1))
                    pool.wait_ge(s_slot_ok, g - 1)
                    settle(pool)
                    scatter(u, 0)
                if fetch:
                    deviation(g + 2, 0)
                if late:
                    scatter(u, 1)

            pool.memset(g_zero[:, :], 0.0).then_inc(s_g_z, 1)
            pool.memset(out_zero[:, :, :], 0.0).then_inc(s_z_pad, 1)
            pool.memset(pad_rows[:, :, :], 0.0).then_inc(s_pad_tok, 1)
            pool.wait_ge(s_ids_ok, 1)
            gather(0, 0)
            gather(0, 1)
            deviation(0, 0)
            pipeline(pool, step)

            for w in range(4):
                pool.wait_ge(out_st[w], 8 * B + FREE)
            pool.wait_ge(s_m_ok, 1)

            def tile(i, u):
                j = 2 * i + u
                pool.wait_ge(s_t_osum, 2 * j + 4)
                pool.wait_ge(s_t_w, j + 3)
                settle(pool)
                for b in range(2):
                    pool.tensor_scalar(oy[u][:, b, :], osum[u][:, b, :], wfin[u][:, b:b + 1], None, ALU.mult)\
                        .then_inc(s_t_oy, 1)
                pool.wait_ge(s_t_oy, 2 * j + 6)
                pool.wait_ge(out_add, 32 * j + ADD_FREE)
                settle(pool)
                for b in range(2):
                    pool.indirect_dma_start(out[:, :], bass.IndirectOffsetOnAxis(ap=dest[u][:, b:b + 1], axis=0),
                                            oy[u][:, b, :], None, compute_op=ALU.add).then_inc(out_add, 16)

            over_tiles(pool, tile)

        @block.scalar
        def _(act):
            act.wait_ge(s_w_bias, 32)
            act.activation(v_s[:, 0:2, :], wst[:, :, 2 * D:3 * D], ACT.Copy, scale=WSCALE).then_inc(s_v_h, 1)
            act.wait_ge(s_w_a, 1)
            act.activation(a_s[:, 0:2, :], ps_q[:, :, 0:2 * P], ACT.Copy, scale=WSCALE / D ** 0.5).then_inc(s_w_ah, 1)
            act.wait_ge(s_g_bias, 32)
            act.activation(g_s[:, 0:2, :], g_st[:, :, :], ACT.Copy, scale=WSCALE).then_inc(s_g_h, 1)

            def step(i, n, fetch, rows, attend, route, late):
                g, u, b = 4 * i + n, n % 2, 2 * i + n // 2
                v = 1 - u
                states = list(range(4 * u, min(4 * u + 4, 7)))

                def state(k):
                    act.wait_ge(s_s32_ok, 7 * b + k + 1)
                    act.copy(ss[k % CH][:, 0:2, 0:D], s32[:, :, :]).then_inc(s_sh_ok, 1)

                def normalise(g, n, src, dst):
                    shift_ok, xn_ok = ((s_shift_ok, s_xn_ok), (s_shift2_ok, s_x2n_ok))[n]
                    act.wait_ge(shift_ok, g + 1)
                    for c in range(CH):
                        act.activation(dst[:, c, 0:D - 1], src[:, c, 0:D - 1], ACT.Identity, bias=shift[n][:, c:c + 1],
                                       scale=rstd[n][:, c:c + 1]).then_inc(xn_ok, 1)

                def high_sums(a):
                    act.wait_ge(s_z_done, CH * g + 2 * a + 2)
                    act.copy(zs[:, 0:2, 2 * a * P:2 * (a + 1) * P], ps_z[a]).then_inc(s_zh_ok, 1)

                if attend:
                    ge(act, s_z_done, CH * g)
                    for a in range(2):
                        act.wait_ge(s_q_full, 2 * g + a + 1)
                        act.activation(qs[:, a, :], ps_q[:, a, :], ACT.Copy, scale=1.0 / WSCALE).then_inc(s_qh_ok, 1)
                if rows:
                    ge(act, s_xl_ok, 2 * g)
                    normalise(g + 1, 0, hr[(n + 1) % 4], xn[v])
                if attend:
                    for a in range(2):
                        act.wait_ge(s_pt_ok, 2 * g + a + 1)
                        act.copy(ps[:, 0, 2 * a:2 * a + 2, :], pt[:, 2 * a:2 * a + 2, :]).then_inc(s_ph_ok, 1)
                    state(states[0])
                if rows:
                    act.wait_ge(s_xn_ok, CH * g + 2 * CH)
                    ge(act, s_z_done, CH * g)
                    act.activation(xs[v][:, :, 0:D - 1], xn[v][:, :, 0:D - 1], ACT.Copy).then_inc(s_xh_ok, 1)
                if late:
                    act.wait_ge(s_tp2_full, g - 1)
                    act.copy(x2t[:, :, :], ps_t[:, 0:3, :]).then_inc(s_tp2_a, 1)
                if attend:
                    state(states[1])
                    ge(act, s_a_full, 2 * g)
                    high_sums(0)
                if late:
                    act.wait_ge(s_gap_ok, g - 1)
                    act.activation(egap[:, :], gap[:, :], ACT.Exp, scale=1.0 / WSCALE).then_inc(s_egap_ok, 1)
                if attend:
                    state(states[2])
                if rows:
                    act.wait_ge(s_tp_full, g + 2)
                    act.copy(xt[v][:, :, :], ps_t[:, 0:3, :]).then_inc(s_tp_a, 1)
                if attend:
                    high_sums(1)
                if route and not late:
                    act.wait_ge(out_add, ADD_FREE)
                if route:
                    ge(act, s_x2l_ok, 2 * (g - 1))
                    normalise(g - 1, 1, hr[(n - 1) % 4], x2n)
                    act.wait_ge(s_x2n_ok, CH * g)
                    act.wait_ge(slot_st[v], 16 * K * CH * (b - 1 + u) + FREE)
                    act.activation(x2s[v][:, :, 0:D - 1], x2n[:, :, 0:D - 1], ACT.Copy).then_inc(s_x2h_ok, 1)
                if attend:
                    for k in states[3:]:
                        state(k)
                if attend and u == 0:
                    act.wait_ge(s_e_bias, 32 * b + 32)
                    act.activation(w1_s[:, bass.ds(b * W1C, 2 * H)], w1_st[:, :, :].rearrange("p a n -> p (a n)"),
                                   ACT.Copy, scale=WSCALE).then_inc(s_e_h1, 1)
                    act.activation(w2_s[:, bass.ds(b * W2C, HM * D)], w2_st[:, :], ACT.Copy, scale=WSCALE)\
                        .then_inc(s_e_h2, 1)

            pipeline(act, step)

            def tile(i, u):
                j = 2 * i + u
                for m in range(HB):
                    act.wait_ge(s_t_h, HB * j + m + 1)
                    act.activation(h32[:, 2 * m:2 * m + 2, :].rearrange("p a b -> p (a b)"), ps_h[m], ACT.Gelu,
                                   scale=1.0 / WSCALE).then_inc(s_t_gelu, 1)
                    act.activation(hs[:, 0, 2 * m:2 * m + 2, :].rearrange("p a b -> p (a b)"), ps_h[m], ACT.Gelu,
                                   scale=1.0 / WSCALE).then_inc(s_t_hh, 1)

            act.wait_ge(s_m_ok, 1)
            over_tiles(act, tile)

        @block.vector
        def _(dve):
            dve.wait_ge(s_x_ld, 16)
            dve.tensor_copy(x_rowsf[:, :], x_rows[:, :]).then_inc(s_xf_ok, 1)
            dve.wait_ge(s_c_ld, 16)
            dve.tensor_copy(ident16[:, :], ident).then_inc(s_c_16, 1)
            dve.tensor_copy(upper16[:, :], cst[:, C_UP:C_UP + P]).then_inc(s_c_16, 1)
            dve.tensor_copy(ones16[:, :], ones).then_inc(s_c_16, 1)
            dve.tensor_copy(tok_i[:, :], cst[:, C_TOK:C_TOK + NCH]).then_inc(s_c_init, 1)
            dve.memset(hotsum[:, :], 0.0).then_inc(s_c_init, 1)
            dve.memset(hotsum16[:, :], 0.0).then_inc(s_c_init, 1)
            dve.wait_ge(s_xtr_full, 1)
            dve.tensor_copy(ids[:, :], ps_g[:, 0:NCH]).then_inc(s_ids_ok, 1)
            dve.wait_ge(s_w_ld, 64)
            for b in range(2):
                dve.tensor_tensor(wst[:, b, :], wst[:, b, :], wlast[:, :], ALU.subtract).then_inc(s_w_sub, 1)
            for u in range(2):
                for c in range(CH):
                    dve.tensor_copy(xn[u][:, c, D - 1:D], row_scale).then_inc(s_c_init, 1)
                dve.memset(x2s[u][:, :, D - 1:D], 1.0).then_inc(s_c_init, 1)
                dve.memset(x2s[u][:, :, 2 * P - 1:2 * P], 0.0).then_inc(s_c_init, 1)
            for c in range(CH):
                dve.memset(ss[c][:, :, :], 0.0).then_inc(s_c_init, 1)
            NINIT = 3 + 2 * (CH + 2) + CH
            dve.wait_ge(s_c_init, NINIT)
            for u in range(2):
                dve.tensor_copy(xs[u][:, :, D - 1:D], xn[u][:, :, D - 1:D]).then_inc(s_c_init, 1)
                dve.wait_ge(s_c_init, NINIT + 2 * u + 1)
                dve.tensor_tensor(xs[u][:, :, 2 * P - 1:2 * P], xn[u][:, :, D - 1:D], xs[u][:, :, D - 1:D], ALU.subtract)\
                    .then_inc(s_c_init, 1)
            dve.wait_ge(s_w_tr, 1)
            for t in range(2):
                for m in range(2):
                    r = (P, D1)[m]
                    dve.tensor_copy(wqk_t[0:r, t, m, 0:D], ps_q[0:r, t, m * 2 * P:m * 2 * P + D]).then_inc(s_w_trc, 1)
                    dve.tensor_copy(wqk_t[0:r, t, m, D:2 * P], ps_q[0:r, t, m * 2 * P + P:m * 2 * P + D])\
                        .then_inc(s_w_trc, 1)
            dve.wait_ge(s_g_ld, 64)
            for b in range(2):
                dve.tensor_tensor(g_st[:, b, :], g_st[:, b, :], g_last[:, :], ALU.subtract).then_inc(s_g_sub, 1)

            def statistics(g, n, src):
                bn_ok, mv_ok = ((s_bn_ok, s_mv_ok), (s_bn2_ok, s_mv2_ok))[n]
                for c in range(CH):
                    dve.bn_stats(st[n][:, c, :], src[:, c, :]).then_inc(bn_ok, 1)
                for c in range(CH):
                    dve.wait_ge(bn_ok, CH * g + c + 1)
                    settle(dve)
                    dve.bn_aggr(mv[n][:, c, :], st[n][:, c, :]).then_inc(mv_ok, 1)

            dve.wait_ge(h_ld[0], 16 * CH)
            statistics(0, 0, hr[0])
            dve.wait_ge(s_v_h, 1)
            dve.scalar_tensor_tensor(v_s[:, 2:4, :], wst[:, :, 2 * D:3 * D], WSCALE, v_s[:, 0:2, :],
                                     ALU.mult, ALU.subtract).then_inc(s_v_l, 1)
            dve.wait_ge(s_w_ah, 1)
            dve.scalar_tensor_tensor(a_s[:, 2:4, :], ps_q[:, :, 0:2 * P], WSCALE / D ** 0.5, a_s[:, 0:2, :],
                                     ALU.mult, ALU.subtract).then_inc(s_w_al, 1)
            dve.wait_ge(s_g_h, 1)
            dve.scalar_tensor_tensor(g_s[:, 2:4, :], g_st[:, :, :], WSCALE, g_s[:, 0:2, :],
                                     ALU.mult, ALU.subtract).then_inc(s_g_l, 1)

            def experts(e, u, part):
                if u == 0:
                    if part < 2:
                        dve.wait_ge(s_e_ld, 80 * e + 80)
                        dve.tensor_tensor(w1_st[:, part, :], w1_st[:, part, :], w1_last[:, :], ALU.subtract)\
                            .then_inc(s_e_sub, 1)
                elif part < 2:
                    dve.wait_ge(s_e_h1, e + 1)
                    dve.scalar_tensor_tensor(w1_s[:, bass.ds(e * W1C + (2 + part) * H, H)], w1_st[:, part, :], WSCALE,
                                             w1_s[:, bass.ds(e * W1C + part * H, H)], ALU.mult, ALU.subtract)\
                        .then_inc(s_e_l1, 1)
                else:
                    dve.wait_ge(s_e_h2, e + 1)
                    dve.scalar_tensor_tensor(w2_s[:, bass.ds(e * W2C + HM * D, HM * D)], w2_st[:, :], WSCALE,
                                             w2_s[:, bass.ds(e * W2C, HM * D)], ALU.mult, ALU.subtract).then_inc(s_e_l2, 1)

            def state(b, k):
                dve.wait_ge(s_s_full, 7 * b + k + 1)
                ge(dve, s_sl_ok, 7 * b + k)
                if k == 0:
                    dve.tensor_copy(s32[:, :, :], ps_s[:, :, 0:D]).then_inc(s_s32_ok, 1)
                else:
                    dve.scalar_tensor_tensor(s32[:, :, :], s32[:, :, :], A128, ps_s[:, :, 0:D],
                                             ALU.mult, ALU.add).then_inc(s_s32_ok, 1)

            def low_state(b, k):
                dve.wait_ge(s_sh_ok, 7 * b + k + 1)
                dve.tensor_tensor(ss[k % CH][:, 2:4, 0:D], s32[:, :, :], ss[k % CH][:, 0:2, 0:D], ALU.subtract)\
                    .then_inc(s_sl_ok, 1)

            def take_logits(g):
                dve.wait_ge(s_lg_full, g + 1)
                dve.tensor_copy(lg[:, :, :], ps_lg).then_inc(s_lg_ok, 1)

            def best_logits(g):
                dve.wait_ge(s_lg_ok, g + 1)
                settle(dve)
                for c in range(CH):
                    dve.max(top[:, c, :], lg[:, c, :]).then_inc(s_top_ok, 1)

            def best_experts(g):
                dve.wait_ge(s_top_ok, CH * g + CH)
                settle(dve)
                for c in range(CH):
                    dve.max_index(topi[:, c, :], top[:, c, :], lg[:, c, :]).then_inc(s_topi_ok, 1)
                dve.tensor_tensor(gap[:, :], top[:, :, 1], top[:, :, 0], ALU.subtract).then_inc(s_gap_ok, 1)

            def expert_numbers(g):
                dve.wait_ge(s_topi_ok, CH * g + CH)
                dve.tensor_copy(topf[:, :, :], topi[:, :, 0:2].rearrange("p c k -> p k c")).then_inc(s_topf_ok, 1)

            def one_hot(g):
                dve.wait_ge(s_topf_ok, g + 1)
                for k in range(K):
                    dve.tensor_tensor(hot[:, k, :, :], topf[:, k, :].unsqueeze(2).to_broadcast([P, CH, E]),
                                      cst[:, C_EX:C_EX + E].unsqueeze(1).to_broadcast([P, CH, E]), ALU.is_equal)\
                        .then_inc(s_hot_ok, 1)

            def both_hot(g):
                dve.wait_ge(s_hot_ok, 2 * g + 2)
                dve.tensor_tensor(hot16[:, :, :], hot[:, 0, :, :], hot[:, 1, :, :], ALU.add).then_inc(s_hot16_ok, 1)
                dve.tensor_tensor(assigned[:, bass.ds(g * CH * E, CH * E)], hot[:, 0, :, :].rearrange("p c e -> p (c e)"),
                                  hot[:, 1, :, :].rearrange("p c e -> p (c e)"), ALU.add).then_inc(s_hot16_ok, 1)

            def weight_sum(g):
                dve.wait_ge(s_egap_ok, g + 1)
                dve.tensor_scalar(egap1[:, :], egap[:, :], 1.0, None, ALU.add).then_inc(s_eg1_ok, 1)

            def first_weight(g):
                dve.wait_ge(s_eg1_ok, g + 1)
                settle(dve)
                dve.reciprocal(prio[:, bass.ds(g * CH, CH)], egap1[:, :]).then_inc(s_wt_ok, 1)

            def row_meta(g, u, b):
                dve.wait_ge(s_wt_ok, 5 * g + 1)
                dve.wait_ge(slot_st[u], 16 * K * CH * b + FREE)
                settle(dve)
                dve.tensor_copy(x2f[u][:, :, MF + 1], prio[:, bass.ds(g * CH, CH)]).then_inc(s_wt_ok, 1)
                dve.tensor_tensor(x2f[u][:, :, MF + 2], egap[:, :], prio[:, bass.ds(g * CH, CH)], ALU.mult)\
                    .then_inc(s_wt_ok, 1)
                dve.tensor_copy(x2f[u][:, :, MF + 3], topf[:, 0, :]).then_inc(s_wt_ok, 1)
                dve.tensor_copy(x2i[u][:, :, MF], tok_i[:, bass.ds(g * CH, CH)]).then_inc(s_wt_ok, 1)

            def expert_places(g):
                dve.wait_ge(s_pl_full, g + 1)
                dve.tensor_tensor(place[:, :, :], ps_pl, cst[:, C_REG:C_REG + E].unsqueeze(1).to_broadcast([P, CH, E]),
                                  ALU.add).then_inc(s_place_ok, 1)
                dve.tensor_reduce(hotred[:, :], hot16[:, :, :].rearrange("p c e -> p e c"), AX.X, ALU.add)\
                    .then_inc(s_hred_ok, 1)
                dve.wait_ge(s_place_ok, g + 1)
                for k in range(K):
                    dve.tensor_tensor(placed[:, k, :, :], hot[:, k, :, :], place[:, :, :], ALU.mult)\
                        .then_inc(s_placed_ok, 1)
                dve.wait_ge(s_hred_ok, g + 1)
                dve.tensor_tensor(hotsum[:, :], hotsum[:, :], hotred[:, :], ALU.add).then_inc(s_hsum_ok, 1)

            def own_places(g, u):
                dve.wait_ge(s_placed_ok, 2 * g + 2)
                dve.tensor_reduce(slotf[:, :, :], placed[:, :, :, :], AX.X, ALU.add).then_inc(s_slotf_ok, 1)
                dve.wait_ge(s_hsum_ok, g + 1)
                dve.tensor_copy(hotsum16[:, :], hotsum[:, :]).then_inc(s_hs16_ok, 1)
                dve.wait_ge(s_slotf_ok, g + 1)
                dve.tensor_copy(slot[u][:, :, :], slotf[:, :, :]).then_inc(s_slot_ok, 1)

            def step(i, n, fetch, rows, attend, route, late):
                g, u, b = 4 * i + n, n % 2, 2 * i + n // 2
                v = 1 - u

                def low_sums(a):
                    dve.wait_ge(s_zh_ok, 2 * g + a + 1)
                    dve.tensor_tensor(zs[:, 2:4, 2 * a * P:2 * (a + 1) * P], ps_z[a],
                                      zs[:, 0:2, 2 * a * P:2 * (a + 1) * P], ALU.subtract).then_inc(s_zl_ok, 1)

                def outputs(a):
                    dve.wait_ge(s_a_full, 2 * g + a + 1)
                    for c in range(2 * a, 2 * a + 2):
                        dve.scalar_tensor_tensor(hr[n % 4][:, c, :], ps_y[a][:, c % 2, 0:D], out_scale, hr[n % 4][:, c, :],
                                                 ALU.mult, ALU.add).then_inc(s_h2_ok, 1)

                if attend:
                    for a in range(2):
                        dve.wait_ge(s_qh_ok, 2 * g + a + 1)
                        dve.scalar_tensor_tensor(qs[:, 2 + a, :], ps_q[:, a, :], 1.0 / WSCALE, qs[:, a, :],
                                                 ALU.mult, ALU.subtract).then_inc(s_ql_ok, 1)
                    state(b, 4 * u)
                if route:
                    dve.wait_ge(s_h2_ok, CH * g)
                    statistics(g - 1, 1, hr[(n - 1) % 4])
                if attend:
                    for a in range(2):
                        dve.wait_ge(s_p_full, g + 1)
                        dve.tensor_tensor(pt[:, 2 * a:2 * a + 2, :], ps_p[:, 2 * a:2 * a + 2, :],
                                          tri.unsqueeze(1).to_broadcast([P, 2, P]), ALU.mult).then_inc(s_pt_ok, 1)
                    for a in range(2):
                        dve.wait_ge(s_ph_ok, 2 * g + a + 1)
                        dve.tensor_tensor(ps[:, 1, 2 * a:2 * a + 2, :], pt[:, 2 * a:2 * a + 2, :],
                                          ps[:, 0, 2 * a:2 * a + 2, :], ALU.subtract).then_inc(s_pl_ok, 1)
                    low_state(b, 4 * u)
                    state(b, 4 * u + 1)
                    experts(b, u, 0)
                if late:
                    take_logits(g - 2)
                if attend:
                    low_state(b, 4 * u + 1)
                if late:
                    best_logits(g - 2)
                if attend:
                    low_sums(0)
                if late:
                    best_experts(g - 2)
                if attend:
                    state(b, 4 * u + 2)
                if late:
                    expert_numbers(g - 2)
                    one_hot(g - 2)
                if attend:
                    low_state(b, 4 * u + 2)
                if late:
                    both_hot(g - 2)
                    weight_sum(g - 2)
                if attend:
                    experts(b, u, 1)
                if late:
                    first_weight(g - 2)
                if attend:
                    experts(b, u, 2)
                if late:
                    row_meta(g - 2, u, b - 1)
                    expert_places(g - 2)
                if attend:
                    low_sums(1)
                if late:
                    own_places(g - 2, u)
                if attend and u == 0:
                    state(b, 3)
                if fetch:
                    dve.wait_ge(h_ld[(n + 2) % 4], 16 * CH * (i + (n + 2) // 4 + 1))
                    dve.wait_ge(s_rstd_ok, g + 2)
                    statistics(g + 2, 0, hr[(n + 2) % 4])
                if attend:
                    outputs(0)
                    if u == 0:
                        low_state(b, 3)
                    outputs(1)
                if route:
                    dve.wait_ge(s_x2h_ok, g)
                    dve.tensor_tensor(x2s[v][:, :, 2 * P:3 * P], x2n[:, :, 0:P], x2s[v][:, :, 0:P], ALU.subtract)\
                        .then_inc(s_x2l_ok, 1)
                    dve.tensor_tensor(x2s[v][:, :, D:D + D1 - 1], x2n[:, :, P:D - 1], x2s[v][:, :, P:D - 1],
                                      ALU.subtract).then_inc(s_x2l_ok, 1)

            pipeline(dve, step)

            done = [0]

            def link(ins):
                done[0] += 1
                ins.then_inc(s_n_ok, 1)
                dve.wait_ge(s_n_ok, done[0])

            def by_tile(ap):
                return ap.unsqueeze(1).to_broadcast([P, NTAB, E])

            def by_expert(ap):
                return ap.unsqueeze(2).to_broadcast([P, NTAB, E])

            tab_n = cst[:, C_TAB:C_TAB + NTAB]
            dve.wait_ge(s_n_full, 1)
            link(dve.tensor_copy(cnt[:, :], ps_n))
            link(dve.tensor_tensor(padf[:, :], cnt[:, :], cst[:, C_REG:C_REG + E], ALU.add))
            dve.tensor_copy(pad_i[:, :], padf[:, :]).then_inc(s_pad_ok, 1)
            link(dve.memset(limit[:, :], 0.0))
            link(dve.memset(limit_tok[:, :], 0.0))
            link(dve.memset(tab[:, :, :], 0.0))
            link(dve.tensor_scalar(tiles_i[:, :], cnt[:, :], TM / 2 - 0.75, 1.0 / TM, ALU.add, ALU.mult))
            link(dve.tensor_copy(tiles_f[:, :], tiles_i[:, :]))
            link(dve.tensor_tensor_scan(ends[:, :], ones[:, 0:E], tiles_f[:, :], 0.0, ALU.mult, ALU.add))
            link(dve.tensor_tensor(past[:, :, :], by_expert(tab_n), by_tile(ends[:, :]), ALU.is_ge))
            link(dve.tensor_reduce(tab_e[:, :], past[:, :, :], AX.X, ALU.add))
            link(dve.tensor_tensor(prod[:, :, :], past[:, :, :], by_tile(tiles_f[:, :]), ALU.mult))
            link(dve.tensor_reduce(tab_start[:, :], prod[:, :, :], AX.X, ALU.add))
            link(dve.tensor_tensor(tab_off[:, :], tab_n, tab_start[:, :], ALU.subtract))
            link(dve.tensor_scalar(tab_row0[:, :], tab_e[:, :], float(E) - 0.5, float(TM), ALU.is_lt, ALU.mult))
            link(dve.tensor_tensor(tab_offv[:, :], tab_off[:, :], tab_row0[:, :], ALU.mult))
            link(dve.scalar_tensor_tensor(tab_row[:, :], tab_e[:, :], float(REGION), tab_offv[:, :], ALU.mult, ALU.add))
            link(dve.tensor_copy(tab_row_i[:, :], tab_row[:, :]))
            link(dve.tensor_scalar(tab_ew[:, :], tab_e[:, :], float(E - 1), None, ALU.min))
            link(dve.tensor_copy(tab_e_i[:, :], tab_ew[:, :]))
            link(dve.tensor_scalar(live[:, :], tab_e[:, SURE:NT].rearrange("p (t u) -> p t u", u=2)[:, :, 0],
                                   float(E) - 0.5, None, ALU.is_lt))
            link(dve.tensor_copy(live_i[:, :], live[:, :]))
            dve.sem_inc(s_m_ok, 1)
            link(dve.tensor_copy(tab[:, :, 0], tab_e[:, :]))
            link(dve.tensor_reduce(over[:, 0:1], cnt[:, :], AX.X, ALU.max))
            link(dve.tensor_scalar(over[:, 1:2], over[:, 0:1], float(CAP), None, ALU.is_gt))
            link(dve.tensor_copy(over_i[:, :], over[:, 1:2]))
            dve.sem_inc(s_over_ok, 1)

            for w in range(4):
                dve.wait_ge(out_st[w], 8 * B + FREE)
            too_many = dve.value_load(over_i[0:1, 0:1], min_val=0, max_val=1)
            with dve.If(too_many != 0):
                def by_chunk(ap):
                    return ap.unsqueeze(2).to_broadcast([P, E, NCH])

                n0 = [0]

                def order(ins):
                    n0[0] += 1
                    ins.then_inc(s_b_ok, 1)
                    dve.wait_ge(s_b_ok, n0[0])

                order(dve.tensor_tensor(pm[:, :, :], assigned[:, :].rearrange("p (c e) -> p e c", e=E),
                                        prio[:, :].unsqueeze(1).to_broadcast([P, E, NCH]), ALU.mult))
                order(dve.memset(limit[:, :], 0.5))
                order(dve.memset(move[:, 0:1], 0.5))
                base = n0[0]
                NP = 24
                with dve.Fori(0, NP) as r:
                    STEPS = 7
                    at = base + r * STEPS
                    dve.tensor_scalar(cand[:, :], limit[:, :], move[:, 0:1], None, ALU.add).then_inc(s_b_ok, 1)
                    dve.wait_ge(s_b_ok, at + 1)
                    dve.tensor_tensor(cmp[:, :, :], pm[:, :, :], by_chunk(cand[:, :]), ALU.is_ge).then_inc(s_b_ok, 1)
                    dve.wait_ge(s_b_ok, at + 2)
                    dve.tensor_reduce(part_cnt[:, :], cmp[:, :, :], AX.X, ALU.add).then_inc(s_b_part, 1)
                    dve.wait_ge(s_b_tot, r + 1)
                    dve.tensor_scalar(took[:, :], ps_n, float(CAP), None, ALU.is_ge).then_inc(s_b_ok, 1)
                    dve.wait_ge(s_b_ok, at + 3)
                    dve.tensor_scalar(cand[:, :], took[:, :], move[:, 0:1], None, ALU.mult).then_inc(s_b_ok, 1)
                    dve.wait_ge(s_b_ok, at + 4)
                    dve.tensor_tensor(limit[:, :], limit[:, :], cand[:, :], ALU.add).then_inc(s_b_ok, 1)
                    dve.tensor_scalar(move[:, 1:2], move[:, 0:1], 0.5, None, ALU.mult).then_inc(s_b_ok, 1)
                    dve.wait_ge(s_b_ok, at + 6)
                    dve.tensor_copy(move[:, 0:1], move[:, 1:2]).then_inc(s_b_ok, 1)
                    dve.wait_ge(s_b_ok, at + 7)
                n0[0] = base + NP * 7
                order(dve.tensor_tensor(cmp[:, :, :], pm[:, :, :], by_chunk(limit[:, :]), ALU.is_gt))
                dve.tensor_reduce(part_cnt[:, :], cmp[:, :, :], AX.X, ALU.add).then_inc(s_b_part, 1)
                dve.wait_ge(s_b_tot, NP + 1)
                order(dve.tensor_scalar(room[:, :], ps_n, -1.0, float(CAP), ALU.mult, ALU.add))
                order(dve.tensor_tensor(tie[:, :, :], pm[:, :, :], by_chunk(limit[:, :]), ALU.is_equal))
                order(dve.memset(move[:, 0:1], float(T)))
                base = n0[0]
                NK = T.bit_length()
                with dve.Fori(0, NK) as r:
                    at = base + r * 8
                    dve.tensor_scalar(cand[:, :], limit_tok[:, :], move[:, 0:1], None, ALU.add).then_inc(s_b_ok, 1)
                    dve.wait_ge(s_b_ok, at + 1)
                    dve.tensor_tensor(cmp[:, :, :], cst[:, C_TOK:C_TOK + NCH].unsqueeze(1).to_broadcast([P, E, NCH]),
                                      by_chunk(cand[:, :]), ALU.is_lt).then_inc(s_b_ok, 1)
                    dve.wait_ge(s_b_ok, at + 2)
                    dve.tensor_tensor(cmp[:, :, :], cmp[:, :, :], tie[:, :, :], ALU.mult).then_inc(s_b_ok, 1)
                    dve.wait_ge(s_b_ok, at + 3)
                    dve.tensor_reduce(part_cnt[:, :], cmp[:, :, :], AX.X, ALU.add).then_inc(s_b_part, 1)
                    dve.wait_ge(s_b_tot, NP + 2 + r)
                    dve.tensor_tensor(took[:, :], ps_n, room[:, :], ALU.is_le).then_inc(s_b_ok, 1)
                    dve.wait_ge(s_b_ok, at + 4)
                    dve.tensor_scalar(cand[:, :], took[:, :], move[:, 0:1], None, ALU.mult).then_inc(s_b_ok, 1)
                    dve.wait_ge(s_b_ok, at + 5)
                    dve.tensor_tensor(limit_tok[:, :], limit_tok[:, :], cand[:, :], ALU.add).then_inc(s_b_ok, 1)
                    dve.tensor_scalar(move[:, 1:2], move[:, 0:1], 0.5, None, ALU.mult).then_inc(s_b_ok, 1)
                    dve.wait_ge(s_b_ok, at + 7)
                    dve.tensor_copy(move[:, 0:1], move[:, 1:2]).then_inc(s_b_ok, 1)
                    dve.wait_ge(s_b_ok, at + 8)

                n0[0] = base + NK * 8
                order(dve.tensor_tensor(past[:, :, :], by_expert(tab_e[:, :]), by_tile(cst[:, C_EX:C_EX + E]),
                                        ALU.is_equal))
                order(dve.tensor_tensor(prod[:, :, :], past[:, :, :], by_tile(limit[:, :]), ALU.mult))
                order(dve.tensor_reduce(tab[:, :, 1], prod[:, :, :], AX.X, ALU.add))
                order(dve.tensor_tensor(prod[:, :, :], past[:, :, :], by_tile(limit_tok[:, :]), ALU.mult))
                order(dve.tensor_reduce(tab[:, :, 2], prod[:, :, :], AX.X, ALU.add))

            dve.sem_inc(s_t_w, 2)
            dve.sem_inc(s_t_osum, 2)
            dve.sem_inc(s_t_oy, 4)
            dve.wait_ge(s_b2_ld, 16 * E)

            def rows_in(j):
                dve.wait_ge(s_t_tp, j + 3)
                dve.tensor_copy(xtt[:, :, :], tview).then_inc(s_t_x, 1)

            rows_in(0)
            def tile(i, u):
                j = 2 * i + u
                for m in range(HB):
                    dve.wait_ge(s_t_gelu, HB * j + m + 1)
                    dve.wait_ge(s_t_hh, HB * j + m + 1 + HB)
                    dve.tensor_tensor(hs[:, 1, 2 * m:2 * m + 2, :], h32[:, 2 * m:2 * m + 2, :],
                                      hs[:, 0, 2 * m:2 * m + 2, :], ALU.subtract).then_inc(s_t_hl, 1)
                    if m == 1:
                        rows_in(j + 1)
                dve.wait_ge(row_ld[u], 16 * i + 16)
                dve.wait_ge(s_t_oy, 2 * j + 2)
                dve.wait_ge(out_add, 32 * (j - 1) + ADD_FREE)
                settle(dve)
                w0, w1_, e0 = xrf[u][:, :, MF + 1], xrf[u][:, :, MF + 2], xrf[u][:, :, MF + 3]
                dve.tensor_copy(tinfo[:, :], tab[:, bass.ds(j, 1), :].rearrange("p a b -> p (a b)"))\
                    .then_inc(s_t_info, 1)
                dve.tensor_copy(wk[:, 0, :], xru[u][:, :, MF]).then_inc(s_t_info, 1)
                dve.tensor_tensor(wk[:, 1, :], w0, w1_, ALU.subtract).then_inc(s_t_info, 1)
                dve.tensor_copy(dest[u][:, :], xru[u][:, :, MF]).then_inc(s_t_info, 1)
                dve.wait_ge(s_t_info, 9 * j + 3)
                dve.scalar_tensor_tensor(wk[:, 2, :], e0, tinfo[:, 0:1], wk[:, 1, :], ALU.is_equal, ALU.mult)\
                    .then_inc(s_t_info, 1)
                dve.tensor_scalar(wk[:, 3, :], wk[:, 0, :], tinfo[:, 2:3], None, ALU.is_lt).then_inc(s_t_info, 1)
                dve.wait_ge(s_t_info, 9 * j + 6)
                dve.tensor_tensor(wk[:, 4, :], wk[:, 2, :], w1_, ALU.add).then_inc(s_t_info, 1)
                dve.scalar_tensor_tensor(wk[:, 5, :], w0, tinfo[:, 1:2], wk[:, 3, :], ALU.is_equal, ALU.mult)\
                    .then_inc(s_t_info, 1)
                dve.wait_ge(s_t_info, 9 * j + 8)
                dve.scalar_tensor_tensor(wk[:, 6, :], w0, tinfo[:, 1:2], wk[:, 5, :], ALU.is_gt, ALU.add)\
                    .then_inc(s_t_info, 1)
                dve.wait_ge(s_t_info, 9 * j + 9)
                dve.tensor_tensor(wfin[u][:, :], wk[:, 4, :], wk[:, 6, :], ALU.mult).then_inc(s_t_w, 1)
                e = dve.value_load(tab_e_i[0:1, bass.ds(j, 1)], min_val=0, max_val=E - 1)
                for b in range(2):
                    dve.wait_ge(s_t_o, j + 1)
                    dve.scalar_tensor_tensor(osum[u][:, b, :], ps_o[b], 1.0 / WSCALE, b2_s[:, bass.ds(e * D, D)],
                                             ALU.mult, ALU.add).then_inc(s_t_osum, 1)

            over_tiles(dve, tile)

        @block.tensor
        def _(pe):
            pe.wait_ge(s_c_ld, 16)
            pe.wait_ge(s_xf_ok, 1)
            pe.transpose(ps_g[:, 0:NCH], x_rowsf[:, :], ident[0:NCH, 0:NCH]).then_inc(s_xtr_full, 1)

            def step(i, n, fetch, rows, attend, route, late):
                g, u, b = 4 * i + n, n % 2, 2 * i + n // 2
                v = 1 - u

                def turn(src, full):
                    for a in range(3):
                        for c in range(CH):
                            last = pe.transpose(ps_t[:, a, c * P:(c + 1) * P], src[:, c, a * P:(a + 1) * P], ident16[:, :])
                    last.then_inc(full, 1)

                def state(k):
                    c = k % CH
                    ge(pe, s_s32_ok, 7 * b + k)
                    for q, (l, r) in enumerate(((0, 0), (2, 0), (0, 1))):
                        lhs = xs[u][:, c, l * P:(l + 1) * P]
                        if r == 0:
                            pe.matmul(ps_s[:, 0, 0:D], lhs, xs[u][:, c, 0:D], start=(q == 0), stop=False)
                        else:
                            pe.matmul(ps_s[:, 0, 0:P], lhs, xs[u][:, c, 2 * P:3 * P], start=False, stop=False)
                            pe.matmul(ps_s[:, 0, P:D], lhs, xs[u][:, c, D:2 * P], start=False, stop=True)
                    lhs = xs[u][:, c, P:2 * P]
                    pe.matmul(ps_s[:, 1, 0:D], lhs, xs[u][:, c, 0:D], start=True, stop=False)
                    pe.matmul(ps_s[:, 1, 0:P], lhs, xs[u][:, c, 2 * P:3 * P], start=False, stop=False)
                    pe.matmul(ps_s[:, 1, P:D], lhs, xs[u][:, c, D:2 * P], start=False, stop=True).then_inc(s_s_full, 1)

                def products(c):
                    for n, (q, r) in enumerate(PASSES):
                        last = pe.matmul(ps_p[:, c, :], xt[u][:, r, c * P:(c + 1) * P], qs[:, q, c * P:(c + 1) * P],
                                         start=(n == 0), stop=(n == 4))
                    if c == CH - 1:
                        last.then_inc(s_p_full, 1)

                def sums(c):
                    k = 4 * u + c
                    ge(pe, s_pl_ok, 2 * g + c // 2 + 1)
                    if k > 0:
                        pe.wait_ge(s_sl_ok, 7 * b + k)
                    for a in range(2):
                        ops = [(xs[u][:, c, 0:P], ps[:, 0, c, :]), (xs[u][:, c, 2 * P:3 * P], ps[:, 0, c, :]),
                               (xs[u][:, c, 0:P], ps[:, 1, c, :])] if a == 0 else \
                              [(xs[u][:, c, P:2 * P], ps[:, 0, c, :]), (xs[u][:, c, P:2 * P], ps[:, 1, c, :])]
                        if k > 0:
                            ops += [(ss[(k - 1) % CH][:, l, a * P:(a + 1) * P], qs[:, q, c * P:(c + 1) * P])
                                    for l, q in PASSES6]
                        for n, (l, r) in enumerate(ops):
                            last = pe.matmul(ps_z[c // 2][:, a, (c % 2) * P:(c % 2 + 1) * P], l, r, start=(n == 0), stop=(n == len(ops) - 1))
                    last.then_inc(s_z_done, 1)

                def output(c):
                    if c % 2 == 0:
                        pe.wait_ge(s_zl_ok, 2 * g + c // 2 + 1)
                        ge(pe, s_h2_ok, CH * g)
                    for n, (w, z) in enumerate(PASSES6):
                        last = pe.matmul(ps_y[c // 2][:, c % 2, 0:D], zs[:, z, c * P:(c + 1) * P], v_s[:, w, :],
                                         start=(n == 0), stop=(n == 5))
                    if c % 2:
                        last.then_inc(s_a_full, 1)

                if attend:
                    pe.wait_ge(s_tp_a, g + 1)
                    ge(pe, s_zl_ok, 2 * g)
                    for a in range(2):
                        for n, (w, r) in enumerate(PASSES):
                            last = pe.matmul(ps_q[:, a, :], a_s[:, w, a * P:(a + 1) * P], xt[u][:, r, :],
                                             start=(n == 0), stop=(n == 4))
                        last.then_inc(s_q_full, 1)
                    state(4 * u)
                if late:
                    pe.wait_ge(s_x2l_ok, 2 * (g - 1))
                    turn(x2s[u], s_tp2_full)
                if attend:
                    pe.wait_ge(s_ql_ok, 2 * g + 2)
                    ge(pe, s_h2_ok, CH * g)
                    for c in range(CH):
                        products(c)
                    state(4 * u + 1)
                    sums(0)
                    sums(1)
                if late:
                    pe.wait_ge(s_tp2_a, g - 1)
                    for c in range(CH):
                        for k, (w, r) in enumerate(PASSES):
                            last = pe.matmul(ps_lg[:, c, :], x2t[:, r, c * P:(c + 1) * P], g_s[:, w, :],
                                             start=(k == 0), stop=(k == 4))
                    last.then_inc(s_lg_full, 1)
                if rows:
                    pe.wait_ge(s_xl_ok, 2 * g + 4)
                    turn(xs[v], s_tp_full)
                if attend:
                    state(4 * u + 2)
                    sums(2)
                    sums(3)
                if late:
                    pe.wait_ge(s_hot16_ok, 2 * (g - 1))
                    for c in range(CH):
                        ops = [(ones16[:, :], hotsum16[:, :])] + [(ones16[:, :], hot16[:, a, :]) for a in range(c)] + \
                              [(upper16[:, :], hot16[:, c, :])]
                        for k, (l, r) in enumerate(ops):
                            last = pe.matmul(ps_pl[:, c, :], l, r, start=(k == 0), stop=(k == len(ops) - 1))
                    last.then_inc(s_pl_full, 1)
                if attend:
                    if u == 0:
                        state(3)
                    output(0)
                    output(1)
                    output(2)
                    output(3)

            def attention_weights():
                pe.wait_ge(s_w_bias, 32)
                for t in range(2):
                    for m in range(2):
                        rm, c0 = (P, D1)[m], t * D + m * P
                        pe.transpose(ps_q[0:rm, t, m * 2 * P:m * 2 * P + P], wst[:, 0, c0:c0 + rm], ident)
                        last = pe.transpose(ps_q[0:rm, t, m * 2 * P + P:m * 2 * P + D], wst[0:D1, 1, c0:c0 + rm],
                                            ident[0:D1, 0:D1])
                last.then_inc(s_w_tr, 1)
                pe.wait_ge(s_w_trc, 8)
                for b in range(2):
                    pe.matmul(ps_q[:, b, 0:2 * P], wqk_t[:, 0, 0, b * P:(b + 1) * P], wqk_t[:, 1, 0, :],
                              start=True, stop=False)
                    last = pe.matmul(ps_q[:, b, 0:2 * P], wqk_t[0:D1, 0, 1, b * P:(b + 1) * P], wqk_t[0:D1, 1, 1, :],
                                     start=False, stop=True)
                last.then_inc(s_w_a, 1)
                pe.wait_ge(s_v_l, 1)
                pe.wait_ge(s_w_al, 1)
                pe.wait_ge(s_g_l, 1)

            attention_weights()
            pe.wait_ge(s_c_16, 3)
            pe.wait_ge(s_c_init, 3 + 2 * (CH + 2) + CH + 4)
            pipeline(pe, step)

            pe.wait_ge(s_hs16_ok, 2 * B)
            pe.matmul(ps_n, ones16[:, :], hotsum16[:, :], start=True, stop=True).then_inc(s_n_full, 1)
            pe.wait_ge(s_over_ok, 1)
            too_many = pe.value_load(over_i[0:1, 0:1], min_val=0, max_val=1)
            with pe.If(too_many != 0):
                with pe.Fori(0, 24 + 1 + T.bit_length()) as r:
                    pe.wait_ge(s_b_part, r + 1)
                    pe.matmul(ps_n, ones, part_cnt[:, :], start=True, stop=True).then_inc(s_b_tot, 1)

            def turn(i, u):
                pe.wait_ge(row_ld[u], 16 * i + 16)
                for a in range(3):
                    for c in range(2):
                        last = pe.transpose(tview[:, a, c * P:(c + 1) * P], xrow[u][:, c, a * P:(a + 1) * P], ident16[:, :])
                last.then_inc(s_t_tp, 1)

            pe.wait_ge(s_m_ok, 1)
            pe.wait_ge(s_e_l1, 2 * E)
            pe.wait_ge(s_e_l2, E)
            pe.sem_inc(s_t_tp, 2)
            pe.sem_inc(s_t_hh, HB)
            pe.wait_ge(s_tp2_a, 2 * B)
            turn(0, 0)
            def tile(i, u):
                j = 2 * i + u
                e = pe.value_load(tab_e_i[0:1, bass.ds(j, 1)], min_val=0, max_val=E - 1)
                pe.wait_ge(s_t_x, j + 1)
                for m in range(HM):
                    if m % 2 == 0:
                        pe.wait_ge(s_t_hh, HB * j + m // 2 + 1)
                    for n, (a, r) in enumerate(PASSES):
                        last = pe.matmul(ps_h[m // 2][:, (m % 2) * TM:(m % 2 + 1) * TM],
                                         w1_s[:, bass.ds(e * W1C + a * H + m * P, P)], xtt[:, r, :],
                                         start=(n == 0), stop=(n == 4))
                    if m % 2:
                        last.then_inc(s_t_h, 1)
                turn(i + u, 1 - u)
                pe.wait_ge(s_t_osum, 2 * j + 2)
                for m in range(HM):
                    if m % 2 == 0:
                        pe.wait_ge(s_t_hl, HB * j + m // 2 + 1)
                    for b in range(2):
                        for n, (v, w) in enumerate(((0, 0), (1, 0), (0, 1))):
                            last = pe.matmul(ps_o[b], hs[:, v, m, b * P:(b + 1) * P],
                                             w2_s[:, bass.ds(e * W2C + w * HM * D + m * D, D)],
                                             start=(m == 0 and n == 0), stop=(m == HM - 1 and n == 2))
                last.then_inc(s_t_o, 1)

            over_tiles(pe, tile)


def kernel(x, L0_tok_weight, L0_attn_W_qkv, L0_attn_b_qkv, L0_ffn_Wg, L0_ffn_W1, L0_ffn_b1, L0_ffn_W2, L0_ffn_b2):
    import concourse.bacc as bacc
    from concourse.bass_utils import run_bass_kernel_spmd

    nc = bacc.Bacc("TRN2", target_bir_lowering=False, num_devices=1)
    B, S = x.shape
    T, D, E = B * S, L0_tok_weight.shape[1], L0_ffn_Wg.shape[1]
    consts = constants(T, E, T + TM, T * 2 // TM + E + 2)
    arrays, args = {}, []
    for name, a in (("x", x), ("emb", L0_tok_weight), ("w_qkv", L0_attn_W_qkv), ("b_qkv", L0_attn_b_qkv),
                    ("wg", L0_ffn_Wg), ("w1", L0_ffn_W1), ("b1", L0_ffn_b1), ("w2", L0_ffn_W2), ("b2", L0_ffn_b2),
                    ("consts", consts)):
        a = np.ascontiguousarray(a)
        arrays["in_" + name] = a
        args.append(nc.dram_tensor("in_" + name, a.shape, mybir.dt.from_np(a.dtype), kind="ExternalInput").ap())
    out = nc.dram_tensor("out_0", (T + TM, D), F32, kind="ExternalOutput").ap()
    lm_tower(nc, *args, out)
    r = run_bass_kernel_spmd(nc, [arrays], core_ids=[0])
    return r.results[0]["out_0"][0:T].reshape(B, S, D)
```
